# Optimizing a Trainium2 kernel written in Bass

```python
import numpy as np
import jax
import jax.numpy as jnp

def _softmax(x, axis=-1):
    return jax.nn.softmax(x, axis=axis)

def _gelu(x):
    return jax.nn.gelu(x, approximate=True)

def _silu(x):
    return jax.nn.silu(x)

def _sigmoid(x):
    return jax.nn.sigmoid(x)

def _layernorm(x, axis=-1, eps=1e-05):
    m = jnp.mean(x, axis=axis, keepdims=True)
    v = jnp.var(x, axis=axis, keepdims=True)
    return (x - m) / jnp.sqrt(v + eps)

def _scatter_add(tgt, idx, src, axis=0):
    return tgt.at[idx].add(src)

def _segment_sum(src, seg, n):
    return jax.ops.segment_sum(src, seg, n)
kernel_name = 'mk_prb_d1_jaxref_r8_35386a'

def setup_inputs(seed: int=0):
    np.random.seed(seed)
    _w = jnp.asarray

    def _L0_attn_setup():
        import jax, jax.numpy as jnp
        import numpy as np
        B, T, V = (4, 512, 128)
        NB = 64
        C = 32
        key = jax.random.key(seed)
        ks = jax.random.split(key, 8)
        return {'x': jax.random.normal(ks[0], (B, T, V), dtype=jnp.float32), 'basis': jax.random.normal(ks[1], (V, 2 * NB), dtype=jnp.float32), 'q_coeffs': jax.random.normal(ks[2], (C, 2 * NB), dtype=jnp.float32) * 0.02, 'k_coeffs': jax.random.normal(ks[3], (C, 2 * NB), dtype=jnp.float32) * 0.02, 'v_coeffs': jax.random.normal(ks[4], (C, 2 * NB), dtype=jnp.float32) * 0.02, 'o_coeffs': jax.random.normal(ks[5], (C, 2 * NB), dtype=jnp.float32) * 0.02, 'decay_logit': jnp.float32(3.0), 'out_scale': jnp.float32(0.1)}
    _L0_attn_in = _L0_attn_setup()

    def _L0_ffn_setup():
        import jax, jax.numpy as jnp
        import numpy as np
        B, S, H, I, E, K = (4, 256, 128, 512, 4, 2)

        def _layer_norm(h, g, b, eps=1e-05):
            mu = h.mean(-1, keepdims=True)
            var = ((h - mu) ** 2).mean(-1, keepdims=True)
            return (h - mu) * jax.lax.rsqrt(var + eps) * g + b
        key = jax.random.key(seed)
        ks = jax.random.split(key, 24)
        rn = lambda k, shape, s=0.02: jax.random.normal(k, shape, dtype=jnp.float32) * s
        z = lambda shape: jnp.zeros(shape, jnp.float32)
        o = lambda shape: jnp.ones(shape, jnp.float32)
        return {'x': rn(ks[0], (B, S, H), 1.0), 'router_w': rn(ks[1], (H, E)), 'router_b': z((E,)), 'load_balancer': o((E,)), 'sw_w1': rn(ks[2], (H, I)), 'sw_w3': rn(ks[3], (H, I)), 'sw_w2': rn(ks[4], (I, H)), 'me_eq_w': rn(ks[5], (H, H)), 'me_eq_b': z((H,)), 'me_wv': rn(ks[6], (H, H)), 'me_bv': z((H,)), 'me_wo': rn(ks[7], (H, H)), 'me_bo': z((H,)), 'me_c1w': rn(ks[8], (H, 2 * H)), 'me_c1b': z((2 * H,)), 'me_c2w': rn(ks[9], (2 * H, H)), 'me_c2b': z((H,)), 'ce_syn_w': rn(ks[10], (H, H)), 'ce_syn_b': z((H,)), 'ce_wv': rn(ks[11], (H, H)), 'ce_bv': z((H,)), 'ce_wo': rn(ks[12], (H, H)), 'ce_bo': z((H,)), 'ce_n1g': o((H,)), 'ce_n1b': z((H,)), 'ce_f1w': rn(ks[13], (H, 2 * H)), 'ce_f1b': z((2 * H,)), 'ce_f2w': rn(ks[14], (2 * H, H)), 'ce_f2b': z((H,)), 'ce_n2g': o((H,)), 'ce_n2b': z((H,)), 'ce_gen_w': rn(ks[15], (H, H)), 'ce_gen_b': z((H,)), 'ml_w1': rn(ks[16], (H, I)), 'ml_b1': z((I,)), 'ml_w2': rn(ks[17], (I, H)), 'ml_b2': z((H,))}
    _L0_ffn_in = _L0_ffn_setup()
    _d = {'L0_attn_x': _L0_attn_in['x'], 'L0_attn_basis': _L0_attn_in['basis'], 'L0_attn_q_coeffs': _L0_attn_in['q_coeffs'], 'L0_attn_k_coeffs': _L0_attn_in['k_coeffs'], 'L0_attn_v_coeffs': _L0_attn_in['v_coeffs'], 'L0_attn_o_coeffs': _L0_attn_in['o_coeffs'], 'L0_attn_decay_logit': _L0_attn_in['decay_logit'], 'L0_attn_out_scale': _L0_attn_in['out_scale'], 'L0_ffn_router_w': _L0_ffn_in['router_w'], 'L0_ffn_router_b': _L0_ffn_in['router_b'], 'L0_ffn_load_balancer': _L0_ffn_in['load_balancer'], 'L0_ffn_sw_w1': _L0_ffn_in['sw_w1'], 'L0_ffn_sw_w3': _L0_ffn_in['sw_w3'], 'L0_ffn_sw_w2': _L0_ffn_in['sw_w2'], 'L0_ffn_me_eq_w': _L0_ffn_in['me_eq_w'], 'L0_ffn_me_eq_b': _L0_ffn_in['me_eq_b'], 'L0_ffn_me_wv': _L0_ffn_in['me_wv'], 'L0_ffn_me_bv': _L0_ffn_in['me_bv'], 'L0_ffn_me_wo': _L0_ffn_in['me_wo'], 'L0_ffn_me_bo': _L0_ffn_in['me_bo'], 'L0_ffn_me_c1w': _L0_ffn_in['me_c1w'], 'L0_ffn_me_c1b': _L0_ffn_in['me_c1b'], 'L0_ffn_me_c2w': _L0_ffn_in['me_c2w'], 'L0_ffn_me_c2b': _L0_ffn_in['me_c2b'], 'L0_ffn_ce_syn_w': _L0_ffn_in['ce_syn_w'], 'L0_ffn_ce_syn_b': _L0_ffn_in['ce_syn_b'], 'L0_ffn_ce_wv': _L0_ffn_in['ce_wv'], 'L0_ffn_ce_bv': _L0_ffn_in['ce_bv'], 'L0_ffn_ce_wo': _L0_ffn_in['ce_wo'], 'L0_ffn_ce_bo': _L0_ffn_in['ce_bo'], 'L0_ffn_ce_n1g': _L0_ffn_in['ce_n1g'], 'L0_ffn_ce_n1b': _L0_ffn_in['ce_n1b'], 'L0_ffn_ce_f1w': _L0_ffn_in['ce_f1w'], 'L0_ffn_ce_f1b': _L0_ffn_in['ce_f1b'], 'L0_ffn_ce_f2w': _L0_ffn_in['ce_f2w'], 'L0_ffn_ce_f2b': _L0_ffn_in['ce_f2b'], 'L0_ffn_ce_n2g': _L0_ffn_in['ce_n2g'], 'L0_ffn_ce_n2b': _L0_ffn_in['ce_n2b'], 'L0_ffn_ce_gen_w': _L0_ffn_in['ce_gen_w'], 'L0_ffn_ce_gen_b': _L0_ffn_in['ce_gen_b'], 'L0_ffn_ml_w1': _L0_ffn_in['ml_w1'], 'L0_ffn_ml_b1': _L0_ffn_in['ml_b1'], 'L0_ffn_ml_w2': _L0_ffn_in['ml_w2'], 'L0_ffn_ml_b2': _L0_ffn_in['ml_b2']}
    _x0 = _d['L0_attn_x']
    _d['L0_attn_x'] = jax.random.normal(jax.random.fold_in(jax.random.key(seed), 1), (16, 512, 128), dtype=_x0.dtype)
    del _x0
    return _d

def reference(L0_attn_x, L0_attn_basis, L0_attn_q_coeffs, L0_attn_k_coeffs, L0_attn_v_coeffs, L0_attn_o_coeffs, L0_attn_decay_logit, L0_attn_out_scale, L0_ffn_router_w, L0_ffn_router_b, L0_ffn_load_balancer, L0_ffn_sw_w1, L0_ffn_sw_w3, L0_ffn_sw_w2, L0_ffn_me_eq_w, L0_ffn_me_eq_b, L0_ffn_me_wv, L0_ffn_me_bv, L0_ffn_me_wo, L0_ffn_me_bo, L0_ffn_me_c1w, L0_ffn_me_c1b, L0_ffn_me_c2w, L0_ffn_me_c2b, L0_ffn_ce_syn_w, L0_ffn_ce_syn_b, L0_ffn_ce_wv, L0_ffn_ce_bv, L0_ffn_ce_wo, L0_ffn_ce_bo, L0_ffn_ce_n1g, L0_ffn_ce_n1b, L0_ffn_ce_f1w, L0_ffn_ce_f1b, L0_ffn_ce_f2w, L0_ffn_ce_f2b, L0_ffn_ce_n2g, L0_ffn_ce_n2b, L0_ffn_ce_gen_w, L0_ffn_ce_gen_b, L0_ffn_ml_w1, L0_ffn_ml_b1, L0_ffn_ml_w2, L0_ffn_ml_b2):

    def _L0_attn_ref(x, basis, q_coeffs, k_coeffs, v_coeffs, o_coeffs, decay_logit, out_scale):
        import jax, jax.numpy as jnp
        import numpy as np
        B, T, V = (4, 512, 128)
        NB = 64
        C = 32
        q_w = basis @ q_coeffs.T
        k_w = basis @ k_coeffs.T
        v_w = basis @ v_coeffs.T
        o_w = basis @ o_coeffs.T
        queries = x @ q_w
        keys = x @ k_w
        values = x @ v_w
        scores = jnp.einsum('btc,bsc->bts', queries, keys)
        decay = jax.nn.sigmoid(decay_logit)
        t = x.shape[1]
        pos = jnp.arange(t)
        diff = pos[None, :] - pos[:, None]
        causal = (diff > 0).astype(x.dtype)
        decay_weights = decay ** jnp.maximum(diff - 1, 0).astype(x.dtype) * causal
        scores = scores * decay_weights[None]
        retrieved = jnp.einsum('bts,bsc->btc', scores, values)
        return retrieved @ o_w.T * out_scale

    def _L0_ffn_ref(x, router_w, router_b, load_balancer, sw_w1, sw_w3, sw_w2, me_eq_w, me_eq_b, me_wv, me_bv, me_wo, me_bo, me_c1w, me_c1b, me_c2w, me_c2b, ce_syn_w, ce_syn_b, ce_wv, ce_bv, ce_wo, ce_bo, ce_n1g, ce_n1b, ce_f1w, ce_f1b, ce_f2w, ce_f2b, ce_n2g, ce_n2b, ce_gen_w, ce_gen_b, ml_w1, ml_b1, ml_w2, ml_b2):
        import jax, jax.numpy as jnp
        import numpy as np
        B, S, H, I, E, K = (4, 256, 128, 512, 4, 2)

        def _layer_norm(h, g, b, eps=1e-05):
            mu = h.mean(-1, keepdims=True)
            var = ((h - mu) ** 2).mean(-1, keepdims=True)
            return (h - mu) * jax.lax.rsqrt(var + eps) * g + b
        logits = jnp.einsum('bsh,he->bse', x, router_w) + router_b + load_balancer
        rw, sel = jax.lax.top_k(logits, K)
        rw = jax.nn.softmax(rw, axis=-1)
        e0 = jax.nn.silu(x @ sw_w1) * (x @ sw_w3) @ sw_w2
        eq = x @ me_eq_w + me_eq_b
        sym = (eq @ me_wv + me_bv) @ me_wo + me_bo
        e1 = jax.nn.gelu(sym @ me_c1w + me_c1b, approximate=False) @ me_c2w + me_c2b
        syn = x @ ce_syn_w + ce_syn_b
        attn = (syn @ ce_wv + ce_bv) @ ce_wo + ce_bo
        h2 = _layer_norm(syn + attn, ce_n1g, ce_n1b)
        ff = jax.nn.relu(h2 @ ce_f1w + ce_f1b) @ ce_f2w + ce_f2b
        h2 = _layer_norm(h2 + ff, ce_n2g, ce_n2b)
        e2 = h2 @ ce_gen_w + ce_gen_b
        e3 = jax.nn.gelu(x @ ml_w1 + ml_b1, approximate=False) @ ml_w2 + ml_b2
        stack = jnp.stack([e0, e1, e2, e3], axis=2)
        gathered = jnp.take_along_axis(stack, sel[..., None], axis=2)
        return (rw[..., None] * gathered).sum(axis=2)
    x = L0_attn_x
    xn = _layernorm(x, axis=-1)
    x = x + _L0_attn_ref(xn, L0_attn_basis, L0_attn_q_coeffs, L0_attn_k_coeffs, L0_attn_v_coeffs, L0_attn_o_coeffs, L0_attn_decay_logit, L0_attn_out_scale) + _L0_ffn_ref(xn, L0_ffn_router_w, L0_ffn_router_b, L0_ffn_load_balancer, L0_ffn_sw_w1, L0_ffn_sw_w3, L0_ffn_sw_w2, L0_ffn_me_eq_w, L0_ffn_me_eq_b, L0_ffn_me_wv, L0_ffn_me_bv, L0_ffn_me_wo, L0_ffn_me_bo, L0_ffn_me_c1w, L0_ffn_me_c1b, L0_ffn_me_c2w, L0_ffn_me_c2b, L0_ffn_ce_syn_w, L0_ffn_ce_syn_b, L0_ffn_ce_wv, L0_ffn_ce_bv, L0_ffn_ce_wo, L0_ffn_ce_bo, L0_ffn_ce_n1g, L0_ffn_ce_n1b, L0_ffn_ce_f1w, L0_ffn_ce_f1b, L0_ffn_ce_f2w, L0_ffn_ce_f2b, L0_ffn_ce_n2g, L0_ffn_ce_n2b, L0_ffn_ce_gen_w, L0_ffn_ce_gen_b, L0_ffn_ml_w1, L0_ffn_ml_b1, L0_ffn_ml_w2, L0_ffn_ml_b2)
    return x

_drawn_inputs = setup_inputs


def setup_inputs(seed=0):
    import zlib

    import numpy as np

    out = dict(_drawn_inputs(seed))
    spreads = {'L0_ffn_router_b': (0.0, 0.8),
     'L0_ffn_load_balancer': (1.0, 0.6),
     'L0_ffn_me_eq_b': (0.0, 0.8),
     'L0_ffn_me_bv': (0.0, 0.8),
     'L0_ffn_me_bo': (0.0, 2.0),
     'L0_ffn_me_c1b': (0.0, 2.0),
     'L0_ffn_me_c2b': (0.0, 2.0),
     'L0_ffn_ce_syn_b': (0.0, 2.0),
     'L0_ffn_ce_bv': (0.0, 2.0),
     'L0_ffn_ce_bo': (0.0, 2.0),
     'L0_ffn_ce_n1g': (1.0, 0.6),
     'L0_ffn_ce_n1b': (0.0, 2.0),
     'L0_ffn_ce_f1b': (0.0, 2.0),
     'L0_ffn_ce_f2b': (0.0, 2.0),
     'L0_ffn_ce_n2g': (1.0, 0.6),
     'L0_ffn_ce_n2b': (0.0, 2.0),
     'L0_ffn_ce_gen_b': (0.0, 2.0),
     'L0_ffn_ml_b1': (0.0, 2.0),
     'L0_ffn_ml_b2': (0.0, 2.0)}
    factors = {'L0_ffn_router_w': 8.0,
     'L0_ffn_sw_w1': 8.0,
     'L0_ffn_sw_w3': 8.0,
     'L0_ffn_sw_w2': 8.0,
     'L0_ffn_me_eq_w': 8.0,
     'L0_ffn_me_wv': 8.0,
     'L0_ffn_me_wo': 8.0,
     'L0_ffn_me_c1w': 8.0,
     'L0_ffn_me_c2w': 8.0,
     'L0_ffn_ce_syn_w': 49.815,
     'L0_ffn_ce_wv': 47.562,
     'L0_ffn_ce_wo': 46.484,
     'L0_ffn_ce_f1w': 45.824,
     'L0_ffn_ce_f2w': 34.381,
     'L0_ffn_ce_gen_w': 26.579,
     'L0_ffn_ml_w1': 8.0,
     'L0_ffn_ml_w2': 8.0}
    for name, (base, spread) in spreads.items():
        noise = np.random.default_rng([zlib.crc32(name.encode()), seed]).standard_normal(out[name].shape)
        drawn = base * np.exp(spread * noise) if base else spread * noise
        out[name] = jnp.asarray(drawn.astype(out[name].dtype))
    for name, factor in factors.items():
        out[name] = (out[name] * factor).astype(out[name].dtype)
    return out
```

```python
from contextlib import ExitStack

import concourse.bass as bass
from concourse import mybir

F32 = mybir.dt.float32
F32R = mybir.dt.float32r
I32 = mybir.dt.int32
ALU = mybir.AluOpType
ACT = mybir.ActivationFunctionType
AX = mybir.AxisListType

P = 128
GROUPS = 16
T = 512
NT = T // P
PAIRS = GROUPS // 2
C = 32
E = 4
I = 512
EPS = 1e-5
DMA_INC = 16

LOADS = [
    [("basisT", P), ("qkT", 4 * C), ("vcT", C), ("ocT", C), ("ce_x0", P + 1), ("ce_wv", P), ("ce_wo", P),
     ("router", E), ("gen_w", P)],
    [("sw_w1", I), ("sw_w3", I)],
    [("me_x0", P + 1), ("me_wv", P), ("me_wo", P), ("me_c1w", 2 * P)],
    [("ml_w1", I), ("f1w", 2 * P)],
    [("f2w", 2 * P), ("sw_w2", I), ("me_c2w", 2 * P), ("ml_w2", I)],
]
COL, LOAD_OF, SPAN = {}, {}, []
_at = 0
for _n, _load in enumerate(LOADS):
    _first = _at
    for _name, _width in _load:
        COL[_name] = (_at, _width)
        LOAD_OF[_name] = _n
        _at += _width
    SPAN.append((_first, _at))
WCOLS = _at

VECS = ["me_bv", "me_bo", "me_c1b0", "me_c1b1", "ce_bv", "ce_bo", "n1g", "n1b", "f1b0", "f1b1", "f2b",
        "n2g", "n2b", "ml_b10", "ml_b11", "ml_b12", "ml_b13"]
ROWS = {"me_c2b": (0, P), "ml_b2": (P, P), "gen_b": (2 * P, P), "router_b": (3 * P, E), "balancer": (3 * P + E, E),
        "decay_logit": (3 * P + 2 * E, 1), "out_scale": (3 * P + 2 * E + 1, 1)}
RCOLS = 3 * P + 2 * E + 2

SPLIT = {"w1": 0, "w3": I, "ml": 2 * I, "f1": 3 * I, "me": 3 * I + 2 * P, "qk": 3 * I + 4 * P}
SCOLS = 3 * I + 5 * P

TOKW = 2 * P + E

UNITS = ([f"tok{t}" for t in range(NT)] + ["qk", "c0", "c1", "c2", "c3", "a0", "b0"]
         + [f"sc{t}" for t in range(NT)] + ["a1", "b1", "f1_0", "f1_1", "a2", "b2", "a3", "b3", "f2", "m0", "m1"])
NU = len(UNITS)
BANKS = 4
assert 2 * NU % BANKS == 0


class Group:

    def __init__(self, pair, off):
        self.pair, self.off = pair, off
        self.par = off % 2

    def next(self):
        return Group(self.pair, self.off + 1)

    def prev(self):
        return Group(self.pair, self.off - 1)

    def count(self, per, n):
        return self.pair * (2 * per) + (self.off * per + n)

    def half(self, per, n):
        return self.pair * per + (self.off // 2 * per + n)

    def index(self):
        return self.pair * 2 + self.off

    def bank(self, unit):
        return (NU * self.off + UNITS.index(unit)) % BANKS

    def uses_before(self, unit):
        return self.pair * (2 * NU // BANKS) + (NU * self.off + UNITS.index(unit)) // BANKS


def wait(eng, sem, value):
    if not isinstance(value, int) or value > 0:
        eng.wait_ge(sem, value)


def build(nc: bass.Bass, x: bass.AP, weights: bass.AP, vecs: bass.AP, rows: bass.AP, out: bass.AP):
    with ExitStack() as ctx:
        def sb(name, shape, dt=F32):
            return ctx.enter_context(nc.sbuf_tensor(name, shape, dt))

        def sem(name):
            return ctx.enter_context(nc.semaphore(name))

        W = sb("W", [P, WCOLS])
        VEC = sb("VEC", [P, len(VECS)])
        ROW = sb("ROW", [P, RCOLS])
        WH = sb("WH", [P, SCOLS], F32R)
        WL = sb("WL", [P, SCOLS], F32R)
        tokw = sb("tokw", [P, TOKW])
        tokb = sb("tokb", [P, P + E])
        ident = sb("ident", [P, P])
        center = sb("center", [P, P])
        qk_w = sb("qk_w", [P, 4 * C])
        vT = sb("vT", [C, P])
        oT = sb("oT", [C, P])
        ce_x1 = sb("ce_x1", [P, P + 1])
        ce_x2 = sb("ce_x2", [P, P + 1])
        me_x1 = sb("me_x1", [P, P + 1])
        me_x2 = sb("me_x2", [P, P + 1])
        me_w = sb("me_w", [P, 2 * P])
        me_b = sb("me_b", [P, 2])
        gen_s = sb("gen_s", [P, P])
        gen_c = sb("gen_c", [P, P])
        gen_bias = sb("gen_bias", [P, P])
        bcast = sb("bcast", [P, 2, P])
        sw2h = sb("sw2h", [P, I])
        bias_h = sb("bias_h", [64, 2, P], F32R)
        bias_l = sb("bias_l", [64, 2, P], F32R)
        bias_r = sb("bias_r", [64, 2, T], F32R)
        ones_f = sb("ones_f", [64, P])
        ones_r = sb("ones_r", [64, P], F32R)
        zero_f = sb("zero_f", [64, 2 * T])
        earlier = sb("earlier", [P, E, E])
        minus1 = sb("minus1", [P, NT])
        eps4 = sb("eps4", [P, NT])
        nhalf = sb("nhalf", [P, NT])
        mask = sb("mask", [P, T])
        power = sb("power", [P, 9])
        PW = 2 * P + 1
        expo = sb("expo", [P, PW], I32)
        bit = sb("bit", [P, 7, PW], I32)
        pacc = sb("pacc", [P, PW])
        ptry = sb("ptry", [P, PW])

        X = [sb(f"X{k}", [P, NT, P]) for k in range(2)]
        OUT = [sb(f"OUT{k}", [P, NT, P]) for k in range(2)]
        xn = sb("xn", [P, NT, P])
        xT = [sb(f"xT{k}", [P, T]) for k in range(2)]
        xh = [sb(f"xh{k}", [P, T], F32R) for k in range(2)]
        xl = [sb(f"xl{k}", [P, T], F32R) for k in range(2)]
        z = sb("z", [P, NT, P])
        pl = sb("pl", [P, NT, P + E])
        n1 = sb("n1", [P, NT, P])
        Q = sb("Q", [3 * C, T], F32R)
        K = sb("K", [3 * C, T], F32R)
        pr = sb("pr", [P, NT, T])
        th = sb("th", [P, NT, T])
        gate = sb("gate", [P, 4, T])
        hid0 = sb("hid0", [P, 4, T])
        hid3 = sb("hid3", [P, 4, T])
        hid1 = sb("hid1", [P, 2, T])
        hid2 = sb("hid2", [P, 2, T])
        h2 = sb("h2", [P, T])
        h2h = sb("h2h", [P, T], F32R)
        h2l = sb("h2l", [P, T], F32R)
        u = sb("u", [P, T])
        e2 = sb("e2", [P, NT, P])
        stats = {k: sb(f"stats_{k}", [P, NT, 6]) for k in "xcu"}
        mv = {k: sb(f"mv_{k}", [P, NT, 2]) for k in "xcu"}
        negmean = {k: sb(f"negmean_{k}", [P, NT]) for k in "xc"}
        veps = {k: sb(f"veps_{k}", [P, NT]) for k in "xcu"}
        rstd = {k: sb(f"rstd_{k}", [P, NT]) for k in "xcu"}
        more = sb("more", [P, NT, E, E])
        same = sb("same", [P, NT, E, E])
        rank = sb("rank", [P, NT, E])
        top = sb("top", [P, NT, E])
        topsum = sb("topsum", [P, NT])
        lean = sb("lean", [P, NT, E])
        tlean = sb("tlean", [P, NT, E])
        tlean1 = sb("tlean1", [P, NT, E])
        half = sb("half", [P, NT, E])
        coef = [sb(f"coef{k}", [P, NT, E]) for k in range(2)]

        S = [ctx.enter_context(nc.psum_tensor(f"S{b}", [P, T], F32)) for b in range(BANKS)]
        TR = ctx.enter_context(nc.psum_tensor("TR", [P, T], F32))
        EX = [ctx.enter_context(nc.psum_tensor(f"EX{b}", [P, NT, P], F32)) for b in range(2)]
        ATT = ctx.enter_context(nc.psum_tensor("ATT", [P, NT, P], F32))

        w_loaded = [sem(f"w_loaded{n}") for n in range(len(LOADS))]
        vec_loaded = sem("vec_loaded")
        row_loaded = sem("row_loaded")
        x_loaded = [sem(f"x_loaded{k}") for k in range(2)]
        out_stored = [sem(f"out_stored{k}") for k in range(2)]
        pool_const = sem("pool_const")
        expo_ready = sem("expo_ready")
        decay_tanh = sem("decay_tanh")
        setup_mm = sem("setup_mm")
        setup_took = sem("setup_took")
        setup_dve = sem("setup_dve")
        split_high = sem("split_high")
        setup_done = sem("setup_done")
        unit_ready = sem("unit_ready")
        released = [sem(f"released{b}") for b in range(BANKS)]
        x_stats = sem("x_stats")
        x_normed = sem("x_normed")
        x_turned = sem("x_turned")
        x_high = sem("x_high")
        x_split = sem("x_split")
        qk_high = sem("qk_high")
        qk_split = sem("qk_split")
        z_taken = sem("z_taken")
        c_stats = sem("c_stats")
        c_normed = sem("c_normed")
        c_turned = sem("c_turned")
        h2_ready = sem("h2_ready")
        h2_high = sem("h2_high")
        h2_low = sem("h2_low")
        lean_ready = sem("lean_ready")
        tlean_ready = sem("tlean_ready")
        th_ready = sem("th_ready")
        gate_ready = sem("gate_ready")
        pr_ready = sem("pr_ready")
        att_ready = sem("att_ready")
        att_added = sem("att_added")
        gelu_done = sem("gelu_done")
        relu_done = sem("relu_done")
        u_ready = sem("u_ready")
        u_turned = sem("u_turned")
        u_stats = sem("u_stats")
        u_rstd = sem("u_rstd")
        ex_ready = sem("ex_ready")
        ex_taken = sem("ex_taken")
        e2_scaled = sem("e2_scaled")
        route_step = sem("route_step")
        out_ready = sem("out_ready")

        def w(name, first=0, width=None):
            at, full = COL[name]
            return W[:, at + first:at + first + (full if width is None else width)]

        def vec(name):
            n = VECS.index(name)
            return VEC[:, n:n + 1]

        def row(name):
            at, width = ROWS[name]
            return ROW[:, at:at + width]

        ALL = [S[0], S[1], S[2], S[3], TR, EX[0], EX[1], ATT]
        flat = [b[:, :] if len(b.shape) == 2 else b[:, :, :].rearrange("p t n -> p (t n)") for b in ALL]
        MM = ["qk", "vT", "ce1", "oT", "me1", "ce2", "vo", "me2", "ce", "ce_b", "me", "me_b", "gen", "gen_b"]

        def prod(name, rows_=P, cols=P):
            return flat[MM.index(name) % len(ALL)][0:rows_, 0:cols]

        block = ctx.enter_context(nc.Block())

        def turns(eng, turn, tail):
            turn(Group(0, 0), True, False)
            turn(Group(0, 1), False, False)
            with eng.Fori(1, PAIRS - 1) as i:
                turn(Group(i, 0), False, False)
                turn(Group(i, 1), False, False)
            turn(Group(PAIRS - 1, 0), False, False)
            turn(Group(PAIRS - 1, 1), False, True)
            tail(Group(PAIRS - 1, 1))

        @block.sync
        def _(sp):
            def load_x(g):
                sp.dma_start(X[g.par][:, :, :], x[g.index()].rearrange("(t p) h -> p t h", p=P)) \
                    .then_inc(x_loaded[g.par], DMA_INC)

            load_x(Group(0, 0))
            sp.dma_start(ROW[:, :], rows[0:1, :].broadcast_to([P, RCOLS])).then_inc(row_loaded, DMA_INC)
            sp.dma_start(VEC[:, :], vecs).then_inc(vec_loaded, DMA_INC)
            for n, (a, b) in enumerate(SPAN):
                sp.dma_start(W[:, a:b], weights[:, a:b]).then_inc(w_loaded[n], DMA_INC)
            load_x(Group(0, 1))

            def store(g):
                sp.wait_ge(out_ready, g.count(1, 1))
                sp.dma_start(out[g.index()].rearrange("(t p) h -> p t h", p=P), OUT[g.par][:, :, :]) \
                    .then_inc(out_stored[g.par], DMA_INC)

            def turn(g, first, last):
                if not first:
                    store(g.prev())
                if not (isinstance(g.pair, int) and g.pair == PAIRS - 1):
                    sp.wait_ge(att_added, g.count(1, 1))
                    load_x(Group(g.pair, g.off + 2))

            turns(sp, turn, store)
            for k in range(2):
                sp.wait_ge(out_stored[k], DMA_INC * PAIRS)

        @block.gpsimd
        def _(pool):
            steps = [0]

            def const(ins):
                steps[0] += 1
                ins.then_inc(pool_const, 1)
                pool.wait_ge(pool_const, steps[0])

            pool.iota(expo[:, 0:P], [[-1, P]], base=-1, channel_multiplier=1).then_inc(expo_ready, 1)
            pool.iota(expo[:, P:P + 1], [[0, 1]], base=0, channel_multiplier=1).then_inc(expo_ready, 1)
            pool.iota(expo[:, P + 1:PW], [[-1, P]], base=P - 1, channel_multiplier=0).then_inc(expo_ready, 1)
            const(pool.memset(nhalf[:, :], -0.5))
            const(pool.memset(minus1[:, :], -1.0))
            const(pool.memset(eps4[:, :], EPS))
            const(pool.memset(ident[:, :], 0.0))
            const(pool.affine_select(out=ident[:, :], in_=ident[:, :], compare_op=ALU.not_equal, fill=1.0, base=0,
                                     pattern=[[-1, P]], channel_multiplier=1))
            const(pool.tensor_scalar(center[:, :], ident[:, :], 1.0, -1.0 / P, ALU.mult, ALU.add))
            const(pool.memset(earlier[:, :, :], 0.0))
            for e in range(1, E):
                const(pool.memset(earlier[:, e, 0:e], 1.0))
            const(pool.memset(ones_f[:, :], 1.0))
            const(pool.memset(zero_f[:, :], 0.0))

            def root(k):
                pool.tensor_tensor(veps[k][:, :], mv[k][:, :, 1], eps4[:, :], ALU.add)
                pool.drain()
                return pool.tensor_tensor(rstd[k][:, :], veps[k][:, :], nhalf[:, :], ALU.pow)

            def norm(k, src, dst, done):
                root(k)
                pool.tensor_tensor(negmean[k][:, :], mv[k][:, :, 0], minus1[:, :], ALU.mult)
                pool.drain()
                for t in range(NT):
                    pool.tensor_scalar(dst[:, t, :], src[:, t, 0:P], negmean[k][:, t:t + 1], rstd[k][:, t:t + 1],
                                       ALU.add, ALU.mult).then_inc(done, 1)

            def norm_x(g):
                pool.wait_ge(x_stats, g.count(1, 1))
                norm("x", X[g.par], xn, x_normed)

            norm_x(Group(0, 0))

            def turn(g, first, last):
                pool.wait_ge(c_stats, g.count(1, 1))
                norm("c", pl, n1, c_normed)
                if not last:
                    norm_x(g.next())
                pool.wait_ge(u_stats, g.count(1, 1))
                root("u").then_inc(u_rstd, 1)

            turns(pool, turn, lambda g: None)

        @block.scalar
        def _(act):
            act.wait_ge(row_loaded, DMA_INC)
            act.activation(power[:, 8:9], row("decay_logit"), ACT.Tanh, scale=0.5).then_inc(decay_tanh, 1)
            act.wait_ge(w_loaded[1], DMA_INC)
            act.copy(WH[:, 0:2 * I], w("sw_w1", 0, 2 * I)).then_inc(split_high, 1)
            act.wait_ge(w_loaded[3], DMA_INC)
            act.copy(WH[:, SPLIT["ml"]:SPLIT["ml"] + I + 2 * P], w("ml_w1", 0, I + 2 * P)).then_inc(split_high, 1)

            def take_x(g):
                act.wait_ge(x_turned, g.count(1, 1))
                act.copy(xT[g.par][:, :], TR[:, :])
                act.copy(xh[g.par][:, :], TR[:, :]).then_inc(x_high, 1)

            take_x(Group(0, 0))
            act.wait_ge(setup_done, 1)

            def turn(g, first, last):
                def unit(name):
                    act.wait_ge(unit_ready, g.count(NU, UNITS.index(name) + 1))
                    return S[g.bank(name)], released[g.bank(name)]

                for t in range(NT):
                    tok, _ = unit(f"tok{t}")
                    act.copy(z[:, t, :], tok[:, 0:P]).then_inc(z_taken, 1)
                qk, _ = unit("qk")
                act.copy(Q[0:2 * C, :], qk[0:2 * C, :])
                act.copy(Q[2 * C:3 * C, :], qk[0:C, :])
                act.copy(K[0:2 * C, :], qk[2 * C:4 * C, :])
                act.copy(K[2 * C:3 * C, :], qk[3 * C:4 * C, :]).then_inc(qk_high, 1)
                act.wait_ge(lean_ready, g.count(1, 1))
                act.activation(tlean[:, :, :], lean[:, :, :], ACT.Tanh).then_inc(tlean_ready, 1)
                for j in range(4):
                    c, free = unit(f"c{j}")
                    act.activation(hid3[:, j, :], c[:, :], ACT.Gelu, bias=vec(f"ml_b1{j}")).then_inc(free, 1)
                act.wait_ge(c_turned, g.count(1, 1))
                act.activation(h2[:, :], TR[:, :], ACT.Identity, bias=vec("n1b"), scale=vec("n1g")) \
                    .then_inc(h2_ready, 1)
                act.wait_ge(h2_ready, g.count(1, 1))
                act.copy(h2h[:, :], h2[:, :]).then_inc(h2_high, 1)

                def half_gate(j):
                    a, _ = unit(f"a{j}")
                    act.activation(th[:, j, :], a[:, :], ACT.Tanh, scale=0.5).then_inc(th_ready, 1)

                half_gate(0)
                half_gate(1)
                for j in range(2):
                    f, free = unit(f"f1_{j}")
                    act.activation(hid2[:, j, :], f[:, :], ACT.Relu, bias=vec(f"f1b{j}")).then_inc(free, 1)
                half_gate(2)
                half_gate(3)
                if not last:
                    take_x(g.next())
                for j in range(2):
                    m, free = unit(f"m{j}")
                    act.activation(hid1[:, j, :], m[:, :], ACT.Gelu, bias=me_b[:, j:j + 1]).then_inc(free, 1)

            turns(act, turn, lambda g: None)

        @block.vector
        def _(dve):
            chain = [0]

            def link(ins):
                chain[0] += 1
                ins.then_inc(setup_dve, 1)
                dve.wait_ge(setup_dve, chain[0])

            def x_moments(g):
                dve.wait_ge(x_loaded[g.par], g.half(DMA_INC, DMA_INC))
                for t in range(NT):
                    dve.bn_stats(stats["x"][:, t, :], X[g.par][:, t, :])
                dve.drain()
                for t in range(NT):
                    ins = dve.bn_aggr(mv["x"][:, t, :], stats["x"][:, t, :])
                ins.then_inc(x_stats, 1)

            x_moments(Group(0, 0))

            dve.wait_ge(decay_tanh, 1)
            link(dve.tensor_scalar(power[:, 0:1], power[:, 8:9], 0.5, 0.5, ALU.mult, ALU.add))
            for n in range(1, 9):
                link(dve.tensor_tensor(power[:, n:n + 1], power[:, n - 1:n], power[:, n - 1:n], ALU.mult))

            taken = [0]

            def product(name):
                assert MM[taken[0]] == name
                dve.wait_ge(setup_mm, taken[0] + 1)
                taken[0] += 1

            def took(ins):
                ins.then_inc(setup_took, 1)
                dve.wait_ge(setup_took, taken[0])

            dve.wait_ge(vec_loaded, DMA_INC)
            dve.wait_ge(w_loaded[0], DMA_INC)
            link(dve.tensor_scalar(gen_s[:, :], w("gen_w"), vec("n2g"), None, ALU.mult))
            link(dve.tensor_copy(bcast[:, 1, :], vec("n2b").broadcast_to([P, P])))
            link(dve.tensor_copy(tokw[:, 2 * P:TOKW], w("router")))
            link(dve.tensor_tensor(tokb[:, P:P + E], row("router_b"), row("balancer"), ALU.add))
            product("qk")
            took(dve.tensor_copy(qk_w[:, :], prod("qk", cols=4 * C)))
            product("vT")
            took(dve.tensor_copy(vT[:, :], prod("vT", C)))
            product("ce1")
            dve.tensor_scalar(ce_x1[:, P:P + 1], prod("ce1", cols=P + 1)[:, P:P + 1], vec("ce_bv"), None, ALU.add)
            took(dve.tensor_copy(ce_x1[:, 0:P], prod("ce1")))
            product("oT")
            took(dve.tensor_scalar(oT[:, :], prod("oT", C), row("out_scale")[0:C], None, ALU.mult))
            product("me1")
            dve.tensor_scalar(me_x1[:, P:P + 1], prod("me1", cols=P + 1)[:, P:P + 1], vec("me_bv"), None, ALU.add)
            took(dve.tensor_copy(me_x1[:, 0:P], prod("me1")))
            product("ce2")
            link(dve.tensor_tensor(ce_x2[:, :], prod("ce2", cols=P + 1), w("ce_x0"), ALU.add))
            took(dve.tensor_scalar(ce_x2[:, P:P + 1], ce_x2[:, P:P + 1], vec("ce_bo"), None, ALU.add))
            link(dve.tensor_copy(bcast[:, 0, :], ce_x2[:, P:P + 1].broadcast_to([P, P])))
            product("vo")
            took(dve.tensor_copy(tokw[:, 0:P], prod("vo")))
            product("me2")
            dve.tensor_scalar(me_x2[:, P:P + 1], prod("me2", cols=P + 1)[:, P:P + 1], vec("me_bo"), None, ALU.add)
            took(dve.tensor_copy(me_x2[:, 0:P], prod("me2")))
            product("ce")
            took(dve.tensor_copy(tokw[:, P:2 * P], prod("ce")))
            product("ce_b")
            took(dve.tensor_copy(tokb[:, 0:P], prod("ce_b")))
            product("me")
            took(dve.tensor_copy(me_w[:, :], prod("me", cols=2 * P)))
            product("me_b")
            took(dve.tensor_tensor(me_b[:, :], prod("me_b", cols=2),
                                   VEC[:, VECS.index("me_c1b0"):VECS.index("me_c1b0") + 2], ALU.add))
            product("gen")
            took(dve.tensor_copy(gen_c[:, :], prod("gen")))
            product("gen_b")
            took(dve.tensor_tensor(gen_bias[:, :], prod("gen_b"), row("gen_b"), ALU.add))

            me, qk = SPLIT["me"], SPLIT["qk"]
            dve.tensor_copy(WH[:, me:me + 2 * P], me_w[:, :])
            link(dve.tensor_copy(WH[:, qk:qk + 4 * C], qk_w[:, :]))
            dve.tensor_tensor(WL[:, me:me + 2 * P], me_w[:, :], WH[:, me:me + 2 * P], ALU.subtract)
            dve.tensor_tensor(WL[:, qk:qk + 4 * C], qk_w[:, :], WH[:, qk:qk + 4 * C], ALU.subtract)
            dve.wait_ge(split_high, 1)
            dve.tensor_tensor(WL[:, 0:2 * I], w("sw_w1", 0, 2 * I), WH[:, 0:2 * I], ALU.subtract)
            dve.wait_ge(split_high, 2)
            ml = SPLIT["ml"]
            dve.tensor_tensor(WL[:, ml:ml + I + 2 * P], w("ml_w1", 0, I + 2 * P), WH[:, ml:ml + I + 2 * P],
                              ALU.subtract)
            dve.wait_ge(w_loaded[4], DMA_INC)
            dve.tensor_scalar(sw2h[:, :], w("sw_w2"), 0.5, None, ALU.mult)

            dve.wait_ge(pool_const, POOL_CONSTS)
            dve.tensor_copy(ones_r[:, :], ones_f[:, :])
            dve.tensor_copy(bias_r[:, :, :].rearrange("p b n -> p (b n)"), zero_f[:, :])
            both = ROW[0:64, 0:2 * P].rearrange("p (b n) -> p b n", b=2)
            link(dve.tensor_copy(bias_h[:, :, :], both))
            link(dve.tensor_tensor(bias_l[:, :, :], both, bias_h[:, :, :], ALU.subtract))
            for b in range(2):
                dve.tensor_copy(bias_r[0:1, b, :].rearrange("p (t n) -> p t n", t=NT),
                                bias_h[0:1, b, :].unsqueeze(1).broadcast_to([1, NT, P]))
                link(dve.tensor_copy(bias_r[32:33, b, :].rearrange("p (t n) -> p t n", t=NT),
                                     bias_l[32:33, b, :].unsqueeze(1).broadcast_to([1, NT, P])))

            def x_low(g):
                dve.wait_ge(x_high, g.count(1, 1))
                dve.tensor_tensor(xl[g.par][:, :], TR[:, :], xh[g.par][:, :], ALU.subtract).then_inc(x_split, 1)

            x_low(Group(0, 0))
            dve.wait_ge(x_split, 1)
            dve.tensor_copy(e2[:, 0, 0:1], me_b[:, 0:1]).then_inc(setup_done, 1)

            dve.wait_ge(expo_ready, 3)
            link(dve.memset(pacc[:, :], 1.0))
            for n in range(7):
                ins = dve.tensor_scalar(bit[:, n, :], expo[:, :], n, 1, ALU.logical_shift_right, ALU.bitwise_and)
            link(ins)
            for n in range(7):
                link(dve.tensor_scalar(ptry[:, :], pacc[:, :], power[:, n:n + 1], None, ALU.mult))
                link(dve.copy_predicated(pacc[:, :], bit[:, n, :], ptry[:, :]))
            dve.tensor_scalar(mask[:, 0:P], pacc[:, P + 1:PW], pacc[:, P:P + 1], power[:, 8:9], ALU.mult, ALU.mult)
            dve.tensor_scalar(mask[:, P:2 * P], pacc[:, P + 1:PW], pacc[:, P:P + 1], power[:, 7:8],
                              ALU.mult, ALU.mult)
            dve.tensor_scalar(mask[:, 2 * P:3 * P], pacc[:, P + 1:PW], pacc[:, P:P + 1], None, ALU.mult)
            link(dve.tensor_scalar(ptry[:, 0:P], expo[:, 0:P], 0.0, None, ALU.is_ge))
            link(dve.tensor_tensor(mask[:, 3 * P:T], pacc[:, 0:P], ptry[:, 0:P], ALU.mult))

            def mix(g, n, e, bank):
                dve.wait_ge(ex_ready, g.count(E, n))
                for t in range(NT):
                    ins = dve.scalar_tensor_tensor(out=OUT[g.par][:, t, :], in0=bank[:, t, :],
                                                   scalar=coef[g.par][:, t, e:e + 1], in1=OUT[g.par][:, t, :],
                                                   op0=ALU.mult, op1=ALU.add)
                ins.then_inc(ex_taken, 1)

            def expert1(g):
                dve.wait_ge(ex_taken, g.count(E, 2))
                mix(g, 3, 1, EX[0])

            def expert2_scale(g):
                dve.wait_ge(u_rstd, g.count(1, 1))
                dve.wait_ge(ex_ready, g.count(E, 4))
                for t in range(NT):
                    ins = dve.scalar_tensor_tensor(out=e2[:, t, :], in0=EX[1][:, t, :],
                                                   scalar=rstd["u"][:, t:t + 1], in1=gen_bias[:, :],
                                                   op0=ALU.mult, op1=ALU.add)
                ins.then_inc(ex_taken, 1)

            def expert2_add(g):
                dve.wait_ge(ex_taken, g.count(E, 4))
                for t in range(NT):
                    ins = dve.scalar_tensor_tensor(out=OUT[g.par][:, t, :], in0=e2[:, t, :],
                                                   scalar=coef[g.par][:, t, 2:3], in1=OUT[g.par][:, t, :],
                                                   op0=ALU.mult, op1=ALU.add)
                ins.then_inc(out_ready, 1)

            def turn(g, first, last):
                def unit(name):
                    dve.wait_ge(unit_ready, g.count(NU, UNITS.index(name) + 1))
                    return S[g.bank(name)], released[g.bank(name)]

                for t in range(NT):
                    dve.wait_ge(z_taken, g.count(NT, t + 1))
                    dve.tensor_tensor(pl[:, t, :], S[g.bank(f"tok{t}")][:, P:TOKW], tokb[:, :], ALU.add) \
                        .then_inc(released[g.bank(f"tok{t}")], 1)
                for t in range(NT):
                    b = g.bank(f"tok{t}")
                    dve.wait_ge(released[b], g.uses_before(f"tok{t}") + 1)
                    dve.bn_stats(stats["c"][:, t, :], pl[:, t, 0:P])
                dve.drain()
                for t in range(NT):
                    ins = dve.bn_aggr(mv["c"][:, t, :], stats["c"][:, t, :])
                ins.then_inc(c_stats, 1)

                def silu(j):
                    dve.wait_ge(th_ready, g.count(4, j + 1))
                    a, a_free = S[g.bank(f"a{j}")], released[g.bank(f"a{j}")]
                    dve.scalar_tensor_tensor(out=gate[:, j, :], in0=th[:, j, :], scalar=1.0, in1=a[:, :],
                                             op0=ALU.add, op1=ALU.mult).then_inc(a_free, 1)
                    b, b_free = unit(f"b{j}")
                    dve.wait_ge(a_free, g.uses_before(f"a{j}") + 1)
                    dve.tensor_tensor(hid0[:, j, :], gate[:, j, :], b[:, :], ALU.mult).then_inc(b_free, 1)

                rs = [0]

                def route(ins):
                    rs[0] += 1
                    ins.then_inc(route_step, 1)
                    dve.wait_ge(route_step, g.count(ROUTE_STEPS, rs[0]))

                logit = pl[:, :, P:P + E]
                mine = logit.unsqueeze(3).broadcast_to([P, NT, E, E])
                other = logit.unsqueeze(2).broadcast_to([P, NT, E, E])
                route(dve.tensor_tensor(same[:, :, :, :], other, mine, ALU.is_equal))
                route(dve.tensor_tensor(same[:, :, :, :], same[:, :, :, :],
                                        earlier[:, :, :].unsqueeze(1).broadcast_to([P, NT, E, E]), ALU.mult))
                route(dve.tensor_tensor(more[:, :, :, :], other, mine, ALU.is_gt))
                route(dve.tensor_tensor(more[:, :, :, :], more[:, :, :, :], same[:, :, :, :], ALU.add))
                route(dve.tensor_reduce(rank[:, :, :], more[:, :, :, :], AX.X, ALU.add))
                route(dve.scalar_tensor_tensor(out=top[:, :, :], in0=rank[:, :, :], scalar=1.5, in1=logit,
                                               op0=ALU.is_lt, op1=ALU.mult))
                route(dve.tensor_reduce(topsum[:, :], top[:, :, :], AX.X, ALU.add))
                dve.scalar_tensor_tensor(out=lean[:, :, :], in0=topsum[:, :].unsqueeze(2).broadcast_to([P, NT, E]),
                                         scalar=-0.5, in1=logit, op0=ALU.mult, op1=ALU.add).then_inc(lean_ready, 1)
                route(dve.tensor_scalar(half[:, :, :], rank[:, :, :], 1.5, 0.5, ALU.is_lt, ALU.mult))

                dve.wait_ge(qk_high, g.count(1, 1))
                qk = S[g.bank("qk")]
                dve.tensor_tensor(Q[C:2 * C, :], qk[C:2 * C, :], Q[C:2 * C, :], ALU.subtract).then_inc(qk_split, 1)
                dve.tensor_tensor(K[2 * C:3 * C, :], qk[3 * C:4 * C, :], K[2 * C:3 * C, :], ALU.subtract) \
                    .then_inc(released[g.bank("qk")], 1)

                if not first:
                    expert1(g.prev())
                    expert2_scale(g.prev())
                silu(0)
                for s in range(NT):
                    n = (s + 1) * P
                    sc, free = unit(f"sc{s}")
                    dve.tensor_tensor(pr[:, s, 0:n], sc[:, 0:n], mask[:, T - n:T], ALU.mult).then_inc(free, 1)
                dve.wait_ge(h2_high, g.count(1, 1))
                dve.tensor_tensor(h2l[:, :], h2[:, :], h2h[:, :], ALU.subtract).then_inc(h2_low, 1)
                silu(1)
                if not first:
                    expert2_add(g.prev())
                dve.wait_ge(tlean_ready, g.count(1, 1))
                route(dve.scalar_tensor_tensor(out=coef[g.par][:, :, :], in0=tlean[:, :, :], scalar=1.0,
                                               in1=half[:, :, :], op0=ALU.add, op1=ALU.mult))
                assert rs[0] == ROUTE_STEPS
                silu(2)
                wait(dve, out_stored[g.par], g.half(DMA_INC, 0))
                dve.wait_ge(att_ready, g.count(1, 1))
                dve.tensor_tensor(OUT[g.par][:, :, :], ATT[:, :, :], X[g.par][:, :, :], ALU.add) \
                    .then_inc(att_added, 1)
                silu(3)
                if not last:
                    x_moments(g.next())
                dve.wait_ge(att_added, g.count(1, 1))
                mix(g, 1, 3, EX[0])
                f2, free = unit("f2")
                dve.scalar_tensor_tensor(out=u[:, :], in0=f2[:, :], scalar=vec("f2b"), in1=h2[:, :],
                                         op0=ALU.add, op1=ALU.add).then_inc(free, 1)
                if not last:
                    x_low(g.next())
                dve.wait_ge(ex_taken, g.count(E, 1))
                mix(g, 2, 0, EX[1])
                dve.wait_ge(u_turned, g.count(1, 1))
                for t in range(NT):
                    dve.bn_stats(stats["u"][:, t, :], TR[:, t * P:(t + 1) * P])
                dve.drain()
                for t in range(NT):
                    ins = dve.bn_aggr(mv["u"][:, t, :], stats["u"][:, t, :])
                ins.then_inc(u_stats, 1)

            def tail(g):
                expert1(g)
                expert2_scale(g)
                expert2_add(g)

            turns(dve, turn, tail)

        @block.tensor
        def _(pe):
            done = [0]

            def setup(name, n_out, lhsT, rhs, rows_=P):
                assert MM[done[0]] == name
                if done[0] >= len(ALL):
                    pe.wait_ge(setup_took, done[0] - len(ALL) + 1)
                pe.matmul(prod(name, rows_, n_out), lhsT, rhs, start=True, stop=True).then_inc(setup_mm, 1)
                done[0] += 1

            def after(name):
                pe.wait_ge(setup_took, MM.index(name) + 1)

            pe.wait_ge(w_loaded[0], DMA_INC)
            setup("qk", 4 * C, w("basisT"), w("qkT"))
            setup("vT", P, w("vcT"), w("basisT"), C)
            setup("ce1", P + 1, w("ce_wv"), w("ce_x0"))
            setup("oT", P, w("ocT"), w("basisT"), C)
            pe.wait_ge(w_loaded[2], DMA_INC)
            setup("me1", P + 1, w("me_wv"), w("me_x0"))
            after("ce1")
            setup("ce2", P + 1, w("ce_wo"), ce_x1[:, :])
            after("oT")
            setup("vo", P, vT[:, :], oT[:, :])
            after("me1")
            setup("me2", P + 1, w("me_wo"), me_x1[:, :])
            pe.wait_ge(pool_const, POOL_CONSTS)
            after("ce2")
            setup("ce", P, ce_x2[:, 0:P], ident[:, :])
            pe.wait_ge(setup_dve, CE_BIAS_LINK)
            setup("ce_b", P, bcast[:, 0, :], ident[:, :])
            after("me2")
            setup("me", 2 * P, me_x2[:, 0:P], w("me_c1w"))
            pe.wait_ge(setup_took, MM.index("me_b") - len(ALL) + 1)
            for j in range(2):
                ins = pe.matmul(flat[MM.index("me_b") % len(ALL)][:, j:j + 1], w("me_c1w", j * P, P),
                                me_x2[:, P:P + 1], start=True, stop=True)
            ins.then_inc(setup_mm, 1)
            done[0] += 1
            setup("gen", P, center[:, :], gen_s[:, :])
            setup("gen_b", P, bcast[:, 1, :], w("gen_w"))

            def turn_x(g):
                for t in range(NT):
                    pe.wait_ge(x_normed, g.count(NT, t + 1))
                    ins = pe.transpose(TR[:, t * P:(t + 1) * P], xn[:, t, :], ident[:, :])
                ins.then_inc(x_turned, 1)

            after("gen_b")
            turn_x(Group(0, 0))
            pe.wait_ge(setup_done, 1)

            def second(bank, hidden, n, wname, bias):
                if bias is not None:
                    pe.matmul(bank[:, :, :].rearrange("p t n -> p (t n)"), ones_r[:, :], bias_r[:, bias, :],
                              start=True, stop=False)
                for t in range(NT):
                    for j in range(n):
                        rhs = sw2h[:, j * P:(j + 1) * P] if wname == "sw_w2" else w(wname, j * P, P)
                        ins = pe.matmul(bank[:, t, :], hidden[:, j, t * P:(t + 1) * P], rhs,
                                        start=(bias is None and j == 0),
                                        stop=(j == n - 1 and (bias is None or t == NT - 1)))
                ins.then_inc(ex_ready, 1)

            def tail(g):
                b = g.bank("m1")
                pe.wait_ge(released[b], g.uses_before("m1") + 1)
                pe.wait_ge(ex_taken, g.count(E, 1))
                second(EX[0], hid1, 2, "me_c2w", 0)
                pe.wait_ge(ex_taken, g.count(E, 2))
                for t in range(NT):
                    ins = pe.matmul(EX[1][:, t, :], u[:, t * P:(t + 1) * P], gen_c[:, :], start=True, stop=True)
                ins.then_inc(ex_ready, 1)

            def turn(g, first, last):
                def fill(name):
                    wait(pe, released[g.bank(name)], g.uses_before(name))
                    return S[g.bank(name)]

                def three(name, col, hi, lo):
                    bank = fill(name)
                    wh, wl = WH[:, col:col + P], WL[:, col:col + P]
                    pe.matmul(bank[:, :], wh, hi, start=True, stop=False)
                    pe.matmul(bank[:, :], wh, lo, start=False, stop=False)
                    pe.matmul(bank[:, :], wl, hi, start=False, stop=True).then_inc(unit_ready, 1)

                h, l, full = xh[g.par][:, :], xl[g.par][:, :], xT[g.par]

                pe.wait_ge(x_split, g.count(1, 1))
                for t in range(NT):
                    bank = fill(f"tok{t}")
                    pe.matmul(bank[:, 0:TOKW], full[:, t * P:(t + 1) * P], tokw[:, :], start=True, stop=True) \
                        .then_inc(unit_ready, 1)
                three("qk", SPLIT["qk"], h, l)
                if not first:
                    tail(g.prev())
                for j in range(4):
                    three(f"c{j}", SPLIT["ml"] + j * P, h, l)
                wait(pe, u_stats, g.count(1, 0))
                for t in range(NT):
                    pe.wait_ge(c_normed, g.count(NT, t + 1))
                    ins = pe.transpose(TR[:, t * P:(t + 1) * P], n1[:, t, :], ident[:, :])
                ins.then_inc(c_turned, 1)

                def gates(j):
                    three(f"a{j}", SPLIT["w1"] + j * P, h, l)
                    three(f"b{j}", SPLIT["w3"] + j * P, h, l)

                gates(0)
                pe.wait_ge(qk_split, g.count(1, 1))
                for s in range(NT):
                    bank = fill(f"sc{s}")
                    if s == 0:
                        b = g.bank("qk")
                        pe.wait_ge(released[b], g.uses_before("qk") + 1)
                    pe.matmul(bank[:, 0:(s + 1) * P], K[:, s * P:(s + 1) * P], Q[:, 0:(s + 1) * P],
                              start=True, stop=True).then_inc(unit_ready, 1)
                gates(1)
                pe.wait_ge(h2_low, g.count(1, 1))
                three("f1_0", SPLIT["f1"], h2h[:, :], h2l[:, :])
                three("f1_1", SPLIT["f1"] + P, h2h[:, :], h2l[:, :])
                wait(pe, att_added, g.count(1, 0))
                b = g.bank(f"sc{NT - 1}")
                pe.wait_ge(released[b], g.uses_before(f"sc{NT - 1}") + 1)
                for t in range(NT):
                    for s in range(t, NT):
                        ins = pe.matmul(ATT[:, t, :], pr[:, s, t * P:(t + 1) * P], z[:, s, :],
                                        start=(s == t), stop=(s == NT - 1))
                ins.then_inc(att_ready, 1)
                gates(2)
                gates(3)
                b = g.bank("c3")
                pe.wait_ge(released[b], g.uses_before("c3") + 1)
                wait(pe, ex_taken, g.prev().count(E, 3) if not first else 0)
                second(EX[0], hid3, 4, "ml_w2", 1)
                bank = fill("f2")
                b = g.bank("f1_1")
                pe.wait_ge(released[b], g.uses_before("f1_1") + 1)
                for j in range(2):
                    ins = pe.matmul(bank[:, :], w("f2w", j * P, P), hid2[:, j, :], start=(j == 0), stop=(j == 1))
                ins.then_inc(unit_ready, 1)
                pe.wait_ge(h2_ready, g.count(1, 1))
                if not last:
                    turn_x(g.next())
                b = g.bank("b3")
                pe.wait_ge(released[b], g.uses_before("b3") + 1)
                wait(pe, ex_taken, g.prev().count(E, 4) if not first else 0)
                second(EX[1], hid0, 4, "sw_w2", None)
                three("m0", SPLIT["me"], h, l)
                three("m1", SPLIT["me"] + P, h, l)
                if not last:
                    pe.wait_ge(x_split, g.next().count(1, 1))
                b = g.bank("f2")
                pe.wait_ge(released[b], g.uses_before("f2") + 1)
                for t in range(NT):
                    ins = pe.transpose(TR[:, t * P:(t + 1) * P], u[:, t * P:(t + 1) * P], ident[:, :])
                ins.then_inc(u_turned, 1)

            turns(pe, turn, tail)


ROUTE_STEPS = 9
POOL_CONSTS = 12
CE_BIAS_LINK = 15


def kernel(**inputs):
    import numpy as np
    import concourse.bacc as bacc
    from concourse.bass_utils import run_bass_kernel_spmd

    a = {k[7:] if k.startswith("L0_ffn_") else k: np.asarray(v) for k, v in inputs.items()}

    def chunks(m):
        return np.concatenate([m[j * P:(j + 1) * P] for j in range(m.shape[0] // P)], axis=1)

    basis_t = a["L0_attn_basis"].T
    q, k = a["L0_attn_q_coeffs"].T, a["L0_attn_k_coeffs"].T
    packed = {
        "basisT": basis_t, "qkT": np.concatenate([q, q, k, k], axis=1),
        "vcT": a["L0_attn_v_coeffs"].T, "ocT": a["L0_attn_o_coeffs"].T,
        "ce_x0": np.concatenate([a["ce_syn_w"].T, a["ce_syn_b"][:, None]], axis=1),
        "ce_wv": a["ce_wv"], "ce_wo": a["ce_wo"], "router": a["router_w"], "gen_w": a["ce_gen_w"],
        "sw_w1": a["sw_w1"], "sw_w3": a["sw_w3"],
        "me_x0": np.concatenate([a["me_eq_w"].T, a["me_eq_b"][:, None]], axis=1),
        "me_wv": a["me_wv"], "me_wo": a["me_wo"], "me_c1w": a["me_c1w"],
        "ml_w1": a["ml_w1"], "f1w": a["ce_f1w"],
        "f2w": chunks(a["ce_f2w"]), "sw_w2": chunks(a["sw_w2"]), "me_c2w": chunks(a["me_c2w"]),
        "ml_w2": chunks(a["ml_w2"]),
    }
    weights = np.concatenate([packed[name] for load in LOADS for name, _ in load], axis=1)
    c1b, f1b, mlb = (a[n].reshape(-1, P) for n in ("me_c1b", "ce_f1b", "ml_b1"))
    vecs = {"me_bv": a["me_bv"], "me_bo": a["me_bo"], "me_c1b0": c1b[0], "me_c1b1": c1b[1],
            "ce_bv": a["ce_bv"], "ce_bo": a["ce_bo"], "n1g": a["ce_n1g"], "n1b": a["ce_n1b"],
            "f1b0": f1b[0], "f1b1": f1b[1], "f2b": a["ce_f2b"], "n2g": a["ce_n2g"], "n2b": a["ce_n2b"],
            "ml_b10": mlb[0], "ml_b11": mlb[1], "ml_b12": mlb[2], "ml_b13": mlb[3]}
    row = np.concatenate([a["me_c2b"], a["ml_b2"], a["ce_gen_b"], a["router_b"], a["load_balancer"],
                          a["L0_attn_decay_logit"].reshape(1), a["L0_attn_out_scale"].reshape(1)])
    arrays = {
        "x": np.ascontiguousarray(a["L0_attn_x"]),
        "weights": np.ascontiguousarray(weights),
        "vecs": np.ascontiguousarray(np.stack([vecs[n] for n in VECS], axis=1)),
        "rows": np.ascontiguousarray(row[None, :]),
    }
    nc = bacc.Bacc("TRN2", target_bir_lowering=False, num_devices=1)
    args = [nc.dram_tensor(n, v.shape, mybir.dt.from_np(v.dtype), kind="ExternalInput").ap()
            for n, v in arrays.items()]
    out = nc.dram_tensor("out", (GROUPS, T, P), F32, kind="ExternalOutput").ap()
    build(nc, *args, out)
    r = run_bass_kernel_spmd(nc, [arrays], core_ids=[0])
    return r.results[0]["out"]
```

```python
from contextlib import ExitStack

import concourse.bass as bass
from concourse import mybir

F32 = mybir.dt.float32
F32R = mybir.dt.float32r
I32 = mybir.dt.int32
ALU = mybir.AluOpType
ACT = mybir.ActivationFunctionType
AX = mybir.AxisListType

P = 128
GROUPS = 16
T = 512
NT = T // P
PAIRS = GROUPS // 2
C = 32
E = 4
I = 512
EPS = 1e-5
DMA_INC = 16

LOADS = [
    [("basisT", P), ("qkT", 4 * C), ("vcT", C), ("ocT", C), ("ce_x0", P + 1), ("ce_wv", P), ("ce_wo", P),
     ("router", E), ("gen_w", P)],
    [("sw_w1", I), ("sw_w3", I)],
    [("me_x0", P + 1), ("me_wv", P), ("me_wo", P), ("me_c1w", 2 * P)],
    [("ml_w1", I), ("f1w", 2 * P)],
    [("f2w", 2 * P), ("sw_w2", I), ("me_c2w", 2 * P), ("ml_w2", I)],
]
COL, LOAD_OF, SPAN = {}, {}, []
_at = 0
for _n, _load in enumerate(LOADS):
    _first = _at
    for _name, _width in _load:
        COL[_name] = (_at, _width)
        LOAD_OF[_name] = _n
        _at += _width
    SPAN.append((_first, _at))
WCOLS = _at

VECS = ["me_bv", "me_bo", "me_c1b0", "me_c1b1", "ce_bv", "ce_bo", "n1g", "n1b", "f1b0", "f1b1", "f2b",
        "n2g", "n2b", "ml_b10", "ml_b11", "ml_b12", "ml_b13", "me_c2b", "ml_b2"]
ROWS = {"gen_b": (0, P), "router_b": (P, E), "balancer": (P + E, E), "decay_logit": (P + 2 * E, 1),
        "out_scale": (P + 2 * E + 1, 1)}
RCOLS = P + 2 * E + 2

SPLIT, _at = {}, 0
for _name, _width in (("w1", I), ("w3", I), ("ml", I), ("f1", 2 * P), ("f2", 2 * P), ("sw2", I), ("me2", 2 * P),
                      ("ml2", I), ("me", 2 * P), ("qk", 4 * C)):
    SPLIT[_name] = _at
    _at += _width
SCOLS = _at
WEIGHT_SPLITS = [(SPLIT["w1"], "sw_w1", 2 * I), (SPLIT["ml"], "ml_w1", I + 2 * P), (SPLIT["f2"], "f2w", 2 * P),
                 (SPLIT["sw2"], "sw_w2", I), (SPLIT["me2"], "me_c2w", 2 * P + I)]
EX_BANK = {3: 0, 0: 1, 2: 1, 1: 0}

TOKW = 2 * P + E

UNITS = ([f"tok{t}" for t in range(NT)] + ["qk", "a0", "b0", "c0", "c1", "c2", "c3"]
         + [f"sc{t}" for t in range(NT)] + ["a1", "b1", "f1_0", "f1_1", "a2", "b2", "a3", "b3", "f2", "m0", "m1"])
NU = len(UNITS)
BANKS = 4
assert 2 * NU % BANKS == 0


class Group:

    def __init__(self, pair, off):
        self.pair, self.off = pair, off
        self.par = off % 2

    def next(self):
        return Group(self.pair, self.off + 1)

    def prev(self):
        return Group(self.pair, self.off - 1)

    def count(self, per, n):
        return self.pair * (2 * per) + (self.off * per + n)

    def half(self, per, n):
        return self.pair * per + (self.off // 2 * per + n)

    def index(self):
        return self.pair * 2 + self.off

    def bank(self, unit):
        return (NU * self.off + UNITS.index(unit)) % BANKS

    def uses_before(self, unit):
        return self.pair * (2 * NU // BANKS) + (NU * self.off + UNITS.index(unit)) // BANKS


def wait(eng, sem, value):
    if not isinstance(value, int) or value > 0:
        eng.wait_ge(sem, value)


def build(nc: bass.Bass, x: bass.AP, weights: bass.AP, vecs: bass.AP, rows: bass.AP, out: bass.AP):
    with ExitStack() as ctx:
        def sb(name, shape, dt=F32):
            return ctx.enter_context(nc.sbuf_tensor(name, shape, dt))

        def sem(name):
            return ctx.enter_context(nc.semaphore(name))

        W = sb("W", [P, WCOLS])
        VEC = sb("VEC", [P, len(VECS)])
        ROW = sb("ROW", [P, RCOLS])
        WH = sb("WH", [P, SCOLS], F32R)
        WL = sb("WL", [P, SCOLS], F32R)
        tokw = sb("tokw", [P, TOKW])
        tokb = sb("tokb", [P, P + E])
        ident = sb("ident", [P, P])
        center = sb("center", [P, P])
        me_b = sb("me_b", [P, 2])
        gen_c = sb("gen_c", [P, P])
        gen_bias = sb("gen_bias", [P, P])
        earlier = sb("earlier", [P, E, E])
        minus1 = sb("minus1", [P, NT])
        eps4 = sb("eps4", [P, NT])
        nhalf = sb("nhalf", [P, NT])
        mask = sb("mask", [P, T])
        scaled = sb("scaled", [P, I])
        power = sb("power", [P, 9])

        X = [sb(f"X{k}", [P, NT, P]) for k in range(2)]
        OUT = [sb(f"OUT{k}", [P, NT, P]) for k in range(2)]
        xn = sb("xn", [P, NT, P])
        xT = [sb(f"xT{k}", [P, T]) for k in range(2)]
        xh = [sb(f"xh{k}", [P, T], F32R) for k in range(2)]
        xl = [sb(f"xl{k}", [P, T], F32R) for k in range(2)]
        z = sb("z", [P, NT, P])
        pl = sb("pl", [P, NT, P + E])
        n1 = sb("n1", [P, NT, P])
        Q = sb("Q", [3 * C, T], F32R)
        K = sb("K", [3 * C, T], F32R)
        th = sb("th", [P, NT, T])
        hid, hidh, hidl = ({e: sb(f"{n}{e}", [P, k, T], dt) for e, k in ((0, 4), (3, 4), (1, 2), (2, 2))}
                           for n, dt in (("hid", F32), ("hidh", F32R), ("hidl", F32R)))
        exT = sb("exT", [P, T])
        h2 = sb("h2", [P, T])
        h2h = sb("h2h", [P, T], F32R)
        h2l = sb("h2l", [P, T], F32R)
        u = sb("u", [P, T])
        stats = {k: sb(f"stats_{k}", [P, NT, 6]) for k in "xcu"}
        mv = {k: sb(f"mv_{k}", [P, NT, 2]) for k in "xcu"}
        negmean = {k: sb(f"negmean_{k}", [P, NT]) for k in "xc"}
        veps = {k: sb(f"veps_{k}", [P, NT]) for k in "xcu"}
        rstd = {k: sb(f"rstd_{k}", [P, NT]) for k in "xcu"}
        more = sb("more", [P, NT, E, E])
        same = sb("same", [P, NT, E, E])
        rank = sb("rank", [P, NT, E])
        top = sb("top", [P, NT, E])
        topsum = sb("topsum", [P, NT])
        lean = sb("lean", [P, NT, E])
        tlean = sb("tlean", [P, NT, E])
        tlean1 = sb("tlean1", [P, NT, E])
        half = sb("half", [P, NT, E])
        coef = [sb(f"coef{k}", [P, NT, E]) for k in range(2)]

        def scratch(*shapes):
            with ExitStack() as lent:
                return [lent.enter_context(nc.sbuf_tensor(name, [rows_, cols] if isinstance(cols, int) else
                                                          [rows_, *cols], dt))
                        for name, rows_, cols, dt in shapes]

        PW = 2 * P + 1
        bit, expo, pacc, ptry = scratch(("bit", P, (7, PW), I32), ("expo", P, PW, I32), ("pacc", P, PW, F32),
                                        ("ptry", P, PW, F32))
        gate = sb("gate", [P, 4, T])
        e2 = sb("e2", [P, NT, P])
        sb("rest_of_scratch", [P, 10 * PW - 5 * T + 4 * 8])
        qk_w, vT, oT, ce_x1, ce_x2, me_x1, me_x2, me_w, gen_s, bcast = scratch(
            ("qk_w", P, 4 * C, F32), ("vT", C, P, F32), ("oT", C, P, F32),
            ("ce_x1", P, P + 1, F32), ("ce_x2", P, P + 1, F32), ("me_x1", P, P + 1, F32), ("me_x2", P, P + 1, F32),
            ("me_w", P, 2 * P, F32), ("gen_s", P, P, F32), ("bcast", P, (2, P), F32))
        pr = sb("pr", [P, NT, T])

        S = [ctx.enter_context(nc.psum_tensor(f"S{b}", [P, T], F32)) for b in range(BANKS)]
        TR = ctx.enter_context(nc.psum_tensor("TR", [P, T], F32))
        EX = [ctx.enter_context(nc.psum_tensor(f"EX{b}", [P, NT, P], F32)) for b in range(2)]
        ATT = ctx.enter_context(nc.psum_tensor("ATT", [P, NT, P], F32))

        w_loaded = [sem(f"w_loaded{n}") for n in range(len(LOADS))]
        vec_loaded = sem("vec_loaded")
        row_loaded = sem("row_loaded")
        x_loaded = [sem(f"x_loaded{k}") for k in range(2)]
        out_stored = [sem(f"out_stored{k}") for k in range(2)]
        pool_const = sem("pool_const")
        expo_ready = sem("expo_ready")
        decay_tanh = sem("decay_tanh")
        setup_mm = sem("setup_mm")
        setup_took = sem("setup_took")
        setup_dve = sem("setup_dve")
        split_high = sem("split_high")
        half_done = sem("half_done")
        split_low = sem("split_low")
        decay_step = sem("decay_step")
        setup_done = sem("setup_done")
        unit_ready = sem("unit_ready")
        released = [sem(f"released{b}") for b in range(BANKS)]
        x_stats = sem("x_stats")
        x_normed = sem("x_normed")
        x_turned = sem("x_turned")
        x_high = sem("x_high")
        x_split = sem("x_split")
        qk_high = sem("qk_high")
        qk_split = sem("qk_split")
        z_taken = sem("z_taken")
        c_stats = sem("c_stats")
        c_normed = sem("c_normed")
        c_turned = sem("c_turned")
        h2_ready = sem("h2_ready")
        h2_high = sem("h2_high")
        h2_low = sem("h2_low")
        lean_ready = sem("lean_ready")
        tlean_ready = sem("tlean_ready")
        th_ready = sem("th_ready")
        gate_ready = sem("gate_ready")
        pr_ready = sem("pr_ready")
        att_ready = sem("att_ready")
        att_added = sem("att_added")
        hid_high = {e: sem(f"hid_high{e}") for e in range(E)}
        hid_low = {e: sem(f"hid_low{e}") for e in range(E)}
        ex_summed = sem("ex_summed")
        ex_copied = sem("ex_copied")
        u_ready = sem("u_ready")
        u_turned = sem("u_turned")
        u_stats = sem("u_stats")
        u_rstd = sem("u_rstd")
        ex_ready = sem("ex_ready")
        ex_taken = sem("ex_taken")
        e2_scaled = sem("e2_scaled")
        route_step = sem("route_step")
        out_ready = sem("out_ready")

        def w(name, first=0, width=None):
            at, full = COL[name]
            return W[:, at + first:at + first + (full if width is None else width)]

        def vec(name):
            n = VECS.index(name)
            return VEC[:, n:n + 1]

        def row(name):
            at, width = ROWS[name]
            return ROW[:, at:at + width]

        ALL = [S[0], S[1], S[2], S[3], EX[0], EX[1], ATT]
        flat = [b[:, :] if len(b.shape) == 2 else b[:, :, :].rearrange("p t n -> p (t n)") for b in ALL]
        MM = ["qk", "vT", "ce1", "oT", "me1", "ce2", "vo", "me2", "ce", "ce_b", "me", "me_b", "gen", "gen_b"]

        def prod(name, rows_=P, cols=P):
            return flat[MM.index(name) % len(ALL)][0:rows_, 0:cols]

        block = ctx.enter_context(nc.Block())

        def turns(eng, turn, tail):
            turn(Group(0, 0), True, False)
            turn(Group(0, 1), False, False)
            with eng.Fori(1, PAIRS - 1) as i:
                turn(Group(i, 0), False, False)
                turn(Group(i, 1), False, False)
            turn(Group(PAIRS - 1, 0), False, False)
            turn(Group(PAIRS - 1, 1), False, True)
            tail(Group(PAIRS - 1, 1))

        @block.sync
        def _(sp):
            def load_x(g):
                sp.dma_start(X[g.par][:, :, :], x[g.index()].rearrange("(t p) h -> p t h", p=P)) \
                    .then_inc(x_loaded[g.par], DMA_INC)

            sp.dma_start(ROW[:, :], rows[0:1, :].broadcast_to([P, RCOLS])).then_inc(row_loaded, DMA_INC)
            load_x(Group(0, 0))
            sp.dma_start(VEC[:, :], vecs).then_inc(vec_loaded, DMA_INC)
            for n, (a, b) in enumerate(SPAN):
                sp.dma_start(W[:, a:b], weights[:, a:b]).then_inc(w_loaded[n], DMA_INC)
            load_x(Group(0, 1))

            def store(g):
                sp.wait_ge(out_ready, g.count(1, 1))
                sp.dma_start(out[g.index()].rearrange("(t p) h -> p t h", p=P), OUT[g.par][:, :, :]) \
                    .then_inc(out_stored[g.par], DMA_INC)

            def turn(g, first, last):
                if not first:
                    store(g.prev())
                if not (isinstance(g.pair, int) and g.pair == PAIRS - 1):
                    sp.wait_ge(att_added, g.count(1, 1))
                    load_x(Group(g.pair, g.off + 2))

            turns(sp, turn, store)
            for k in range(2):
                sp.wait_ge(out_stored[k], DMA_INC * PAIRS)

        @block.gpsimd
        def _(pool):
            steps = [0]

            def const(ins):
                steps[0] += 1
                ins.then_inc(pool_const, 1)
                pool.wait_ge(pool_const, steps[0])

            pool.iota(expo[:, 0:P], [[-1, P]], base=-1, channel_multiplier=1).then_inc(expo_ready, 1)
            pool.iota(expo[:, P:P + 1], [[0, 1]], base=0, channel_multiplier=1).then_inc(expo_ready, 1)
            pool.iota(expo[:, P + 1:PW], [[-1, P]], base=P - 1, channel_multiplier=0).then_inc(expo_ready, 1)
            const(pool.memset(nhalf[:, :], -0.5))
            const(pool.memset(minus1[:, :], -1.0))
            const(pool.memset(eps4[:, :], EPS))
            const(pool.memset(ident[:, :], 0.0))
            const(pool.affine_select(out=ident[:, :], in_=ident[:, :], compare_op=ALU.not_equal, fill=1.0, base=0,
                                     pattern=[[-1, P]], channel_multiplier=1))
            const(pool.tensor_scalar(center[:, :], ident[:, :], 1.0, -1.0 / P, ALU.mult, ALU.add))
            const(pool.memset(earlier[:, :, :], 0.0))
            for e in range(1, E):
                const(pool.memset(earlier[:, e, 0:e], 1.0))

            def root(k):
                pool.tensor_tensor(veps[k][:, :], mv[k][:, :, 1], eps4[:, :], ALU.add)
                pool.drain()
                return pool.tensor_tensor(rstd[k][:, :], veps[k][:, :], nhalf[:, :], ALU.pow)

            def norm(k, src, dst, done):
                root(k)
                pool.tensor_tensor(negmean[k][:, :], mv[k][:, :, 0], minus1[:, :], ALU.mult)
                pool.drain()
                for t in range(NT):
                    pool.tensor_scalar(dst[:, t, :], src[:, t, 0:P], negmean[k][:, t:t + 1], rstd[k][:, t:t + 1],
                                       ALU.add, ALU.mult).then_inc(done, 1)

            def norm_x(g):
                pool.wait_ge(x_stats, g.count(1, 1))
                norm("x", X[g.par], xn, x_normed)

            norm_x(Group(0, 0))

            for n, (first_col, name, width) in enumerate(WEIGHT_SPLITS):
                pool.wait_ge(split_high, n + 1)
                src = scaled[:, :] if name == "sw_w2" else w(name, 0, width)
                cols = slice(first_col, first_col + width)
                pool.tensor_tensor(WL[:, cols], src, WH[:, cols], ALU.subtract).then_inc(split_low, 1)

            def turn(g, first, last):
                def low(e, a, b):
                    parts = {3: 3, 2: 1, 0: 3, 1: 1}[e]
                    part = {3: {0: 1, 1: 2, 2: 3}, 0: {0: 1, 2: 2, 3: 3}}.get(e, {0: 1})[a]
                    pool.wait_ge(hid_high[e], g.count(parts, part))
                    for j in range(a, b):
                        pool.tensor_tensor(hidl[e][:, j, :], hid[e][:, j, :], hidh[e][:, j, :], ALU.subtract) \
                            .then_inc(hid_low[e], 1)

                pool.wait_ge(c_stats, g.count(1, 1))
                norm("c", pl, n1, c_normed)
                if not last:
                    norm_x(g.next())
                low(3, 0, 1)
                low(3, 1, 2)
                low(3, 2, 4)
                low(2, 0, 2)
                low(0, 0, 2)
                low(0, 2, 3)
                low(0, 3, 4)
                low(1, 0, 2)
                pool.wait_ge(u_stats, g.count(1, 1))
                root("u").then_inc(u_rstd, 1)

            turns(pool, turn, lambda g: None)

        @block.scalar
        def _(act):
            act.wait_ge(row_loaded, DMA_INC)
            act.activation(power[:, 8:9], row("decay_logit"), ACT.Tanh, scale=0.5).then_inc(decay_tanh, 1)
            def take_x(g):
                act.wait_ge(x_turned, g.count(1, 1))
                act.copy(xT[g.par][:, :], TR[:, :])
                act.copy(xh[g.par][:, :], TR[:, :]).then_inc(x_high, 1)

            def high(n):
                first_col, name, width = WEIGHT_SPLITS[n]
                act.wait_ge(w_loaded[LOAD_OF[name]], DMA_INC)
                src = w(name, 0, width)
                if name == "sw_w2":
                    act.mul(scaled[:, :], src, 0.5).then_inc(half_done, 1)
                    act.wait_ge(half_done, 1)
                    src = scaled[:, :]
                act.copy(WH[:, first_col:first_col + width], src).then_inc(split_high, 1)

            high(0)
            take_x(Group(0, 0))
            for n in range(1, len(WEIGHT_SPLITS)):
                high(n)
            act.wait_ge(setup_done, 1)

            def expert_copy(g, n, e, bias):
                act.wait_ge(ex_summed, g.count(3, n))
                src = EX[EX_BANK[e]][:, :, :].rearrange("p t n -> p (t n)")
                if bias is None:
                    ins = act.copy(exT[:, :], src)
                else:
                    ins = act.activation(exT[:, :], src, ACT.Identity, bias=vec(bias))
                ins.then_inc(ex_copied, 1)

            def turn(g, first, last):
                def unit(name):
                    act.wait_ge(unit_ready, g.count(NU, UNITS.index(name) + 1))
                    return S[g.bank(name)], released[g.bank(name)]

                for t in range(NT):
                    tok, _ = unit(f"tok{t}")
                    act.copy(z[:, t, :], tok[:, 0:P]).then_inc(z_taken, 1)
                qk, _ = unit("qk")
                act.copy(Q[0:2 * C, :], qk[0:2 * C, :])
                act.copy(Q[2 * C:3 * C, :], qk[0:C, :])
                act.copy(K[0:2 * C, :], qk[2 * C:4 * C, :])
                act.copy(K[2 * C:3 * C, :], qk[3 * C:4 * C, :]).then_inc(qk_high, 1)
                if not first:
                    expert_copy(g.prev(), 3, 1, "me_c2b")

                def half_gate(j):
                    a, _ = unit(f"a{j}")
                    act.activation(th[:, j, :], a[:, :], ACT.Tanh, scale=0.5).then_inc(th_ready, 1)

                def high(e, a, b, unit_name):
                    act.wait_ge(released[g.bank(unit_name)], g.uses_before(unit_name) + 1)
                    act.copy(hidh[e][:, a:b, :], hid[e][:, a:b, :]).then_inc(hid_high[e], 1)

                half_gate(0)
                for j in range(4):
                    c, free = unit(f"c{j}")
                    act.activation(hid[3][:, j, :], c[:, :], ACT.Gelu, bias=vec(f"ml_b1{j}")).then_inc(free, 1)
                    if j == 1:
                        high(3, 0, 1, "c0")
                    if j == 3:
                        high(3, 1, 2, "c1")
                act.wait_ge(c_turned, g.count(1, 1))
                act.activation(h2[:, :], TR[:, :], ACT.Identity, bias=vec("n1b"), scale=vec("n1g")) \
                    .then_inc(h2_ready, 1)
                act.wait_ge(h2_ready, g.count(1, 1))
                act.copy(h2h[:, :], h2[:, :]).then_inc(h2_high, 1)
                high(3, 2, 4, "c3")
                act.wait_ge(lean_ready, g.count(1, 1))
                act.activation(tlean[:, :, :], lean[:, :, :], ACT.Tanh).then_inc(tlean_ready, 1)
                half_gate(1)
                for j in range(2):
                    f, free = unit(f"f1_{j}")
                    act.activation(hid[2][:, j, :], f[:, :], ACT.Relu, bias=vec(f"f1b{j}")).then_inc(free, 1)
                high(2, 0, 2, "f1_1")
                high(0, 0, 2, "b1")
                half_gate(2)
                half_gate(3)
                high(0, 2, 3, "b2")
                expert_copy(g, 1, 3, "ml_b2")
                high(0, 3, 4, "b3")
                if not last:
                    take_x(g.next())
                expert_copy(g, 2, 0, None)
                for j in range(2):
                    m, free = unit(f"m{j}")
                    act.activation(hid[1][:, j, :], m[:, :], ACT.Gelu, bias=me_b[:, j:j + 1]).then_inc(free, 1)
                high(1, 0, 2, "m1")

            turns(act, turn, lambda g: expert_copy(g, 3, 1, "me_c2b"))

        @block.vector
        def _(dve):
            chain = [0]

            def link(ins):
                chain[0] += 1
                ins.then_inc(setup_dve, 1)
                dve.wait_ge(setup_dve, chain[0])

            def x_moments(g):
                dve.wait_ge(x_loaded[g.par], g.half(DMA_INC, DMA_INC))
                for t in range(NT):
                    dve.bn_stats(stats["x"][:, t, :], X[g.par][:, t, :])
                dve.drain()
                for t in range(NT):
                    ins = dve.bn_aggr(mv["x"][:, t, :], stats["x"][:, t, :])
                ins.then_inc(x_stats, 1)

            dve.wait_ge(expo_ready, 3)
            dve.memset(pacc[:, :], 1.0)
            for n in range(7):
                dve.tensor_scalar(bit[:, n, :], expo[:, :], n, 1, ALU.logical_shift_right, ALU.bitwise_and)
            x_moments(Group(0, 0))
            dve.wait_ge(decay_tanh, 1)
            decay_at = [0]

            def decay_steps(count):
                for _ in range(count):
                    kind, n = DECAY_STEPS[decay_at[0]]
                    if decay_at[0] > 0:
                        dve.wait_ge(decay_step, decay_at[0])
                    if kind == "power" and n == 0:
                        ins = dve.tensor_scalar(power[:, 0:1], power[:, 8:9], 0.5, 0.5, ALU.mult, ALU.add)
                    elif kind == "power":
                        ins = dve.tensor_tensor(power[:, n:n + 1], power[:, n - 1:n], power[:, n - 1:n], ALU.mult)
                    elif kind == "times":
                        ins = dve.tensor_scalar(ptry[:, :], pacc[:, :], power[:, n:n + 1], None, ALU.mult)
                    else:
                        ins = dve.copy_predicated(pacc[:, :], bit[:, n, :], ptry[:, :])
                    ins.then_inc(decay_step, 1)
                    decay_at[0] += 1

            decay_steps(2)
            taken = [0]

            def product(name):
                assert MM[taken[0]] == name
                dve.wait_ge(setup_mm, taken[0] + 1)
                taken[0] += 1

            def took(ins):
                ins.then_inc(setup_took, 1)
                dve.wait_ge(setup_took, taken[0])

            dve.wait_ge(vec_loaded, DMA_INC)
            dve.wait_ge(w_loaded[0], DMA_INC)
            link(dve.tensor_scalar(gen_s[:, :], w("gen_w"), vec("n2g"), None, ALU.mult))
            link(dve.tensor_copy(bcast[:, 1, :], vec("n2b").broadcast_to([P, P])))
            link(dve.tensor_copy(tokw[:, 2 * P:TOKW], w("router")))
            link(dve.tensor_tensor(tokb[:, P:P + E], row("router_b"), row("balancer"), ALU.add))
            decay_steps(2)
            product("qk")
            took(dve.tensor_copy(qk_w[:, :], prod("qk", cols=4 * C)))
            decay_steps(2)
            product("vT")
            took(dve.tensor_copy(vT[:, :], prod("vT", C)))
            decay_steps(2)
            product("ce1")
            dve.tensor_scalar(ce_x1[:, P:P + 1], prod("ce1", cols=P + 1)[:, P:P + 1], vec("ce_bv"), None, ALU.add)
            took(dve.tensor_copy(ce_x1[:, 0:P], prod("ce1")))
            decay_steps(2)
            product("oT")
            took(dve.tensor_scalar(oT[:, :], prod("oT", C), row("out_scale")[0:C], None, ALU.mult))
            decay_steps(2)
            product("me1")
            dve.tensor_scalar(me_x1[:, P:P + 1], prod("me1", cols=P + 1)[:, P:P + 1], vec("me_bv"), None, ALU.add)
            took(dve.tensor_copy(me_x1[:, 0:P], prod("me1")))
            decay_steps(2)
            product("ce2")
            link(dve.tensor_tensor(ce_x2[:, :], prod("ce2", cols=P + 1), w("ce_x0"), ALU.add))
            took(dve.tensor_scalar(ce_x2[:, P:P + 1], ce_x2[:, P:P + 1], vec("ce_bo"), None, ALU.add))
            link(dve.tensor_copy(bcast[:, 0, :], ce_x2[:, P:P + 1].broadcast_to([P, P])))
            decay_steps(2)
            product("vo")
            took(dve.tensor_copy(tokw[:, 0:P], prod("vo")))
            decay_steps(2)
            product("me2")
            dve.tensor_scalar(me_x2[:, P:P + 1], prod("me2", cols=P + 1)[:, P:P + 1], vec("me_bo"), None, ALU.add)
            took(dve.tensor_copy(me_x2[:, 0:P], prod("me2")))
            decay_steps(2)
            product("ce")
            took(dve.tensor_copy(tokw[:, P:2 * P], prod("ce")))
            decay_steps(1)
            product("ce_b")
            took(dve.tensor_copy(tokb[:, 0:P], prod("ce_b")))
            decay_steps(1)
            product("me")
            took(dve.tensor_copy(me_w[:, :], prod("me", cols=2 * P)))
            decay_steps(1)
            product("me_b")
            took(dve.tensor_tensor(me_b[:, :], prod("me_b", cols=2),
                                   VEC[:, VECS.index("me_c1b0"):VECS.index("me_c1b0") + 2], ALU.add))
            product("gen")
            took(dve.tensor_copy(gen_c[:, :], prod("gen")))
            product("gen_b")
            took(dve.tensor_tensor(gen_bias[:, :], prod("gen_b"), row("gen_b"), ALU.add))

            def x_low(g):
                dve.wait_ge(x_high, g.count(1, 1))
                dve.tensor_tensor(xl[g.par][:, :], TR[:, :], xh[g.par][:, :], ALU.subtract).then_inc(x_split, 1)

            me, qk = SPLIT["me"], SPLIT["qk"]
            dve.tensor_copy(WH[:, me:me + 2 * P], me_w[:, :])
            link(dve.tensor_copy(WH[:, qk:qk + 4 * C], qk_w[:, :]))
            x_low(Group(0, 0))
            dve.tensor_tensor(WL[:, me:me + 2 * P], me_w[:, :], WH[:, me:me + 2 * P], ALU.subtract)
            dve.tensor_tensor(WL[:, qk:qk + 4 * C], qk_w[:, :], WH[:, qk:qk + 4 * C], ALU.subtract) \
                .then_inc(setup_done, 1)

            assert decay_at[0] == len(DECAY_STEPS)
            dve.wait_ge(decay_step, len(DECAY_STEPS))
            dve.tensor_scalar(mask[:, 0:P], pacc[:, P + 1:PW], pacc[:, P:P + 1], power[:, 8:9], ALU.mult, ALU.mult)
            dve.tensor_scalar(mask[:, P:2 * P], pacc[:, P + 1:PW], pacc[:, P:P + 1], power[:, 7:8],
                              ALU.mult, ALU.mult)
            dve.tensor_scalar(mask[:, 2 * P:3 * P], pacc[:, P + 1:PW], pacc[:, P:P + 1], None, ALU.mult)
            link(dve.tensor_scalar(ptry[:, 0:P], expo[:, 0:P], 0.0, None, ALU.is_ge))
            link(dve.tensor_tensor(mask[:, 3 * P:T], pacc[:, 0:P], ptry[:, 0:P], ALU.mult))

            def mix(g, n, e):
                dve.wait_ge(ex_ready, g.count(E, n))
                for t in range(NT):
                    ins = dve.scalar_tensor_tensor(out=OUT[g.par][:, t, :], in0=EX[EX_BANK[e]][:, t, :],
                                                   scalar=coef[g.par][:, t, e:e + 1], in1=OUT[g.par][:, t, :],
                                                   op0=ALU.mult, op1=ALU.add)
                ins.then_inc(ex_taken, 1)

            def expert2_scale(g):
                dve.wait_ge(u_rstd, g.count(1, 1))
                dve.wait_ge(ex_ready, g.count(E, 3))
                for t in range(NT):
                    ins = dve.scalar_tensor_tensor(out=e2[:, t, :], in0=EX[EX_BANK[2]][:, t, :],
                                                   scalar=rstd["u"][:, t:t + 1], in1=gen_bias[:, :],
                                                   op0=ALU.mult, op1=ALU.add)
                ins.then_inc(ex_taken, 1)

            def expert1(g):
                dve.wait_ge(ex_taken, g.count(E, 2))
                mix(g, 4, 1)

            def expert2_add(g):
                dve.wait_ge(ex_taken, g.count(E, 4))
                for t in range(NT):
                    ins = dve.scalar_tensor_tensor(out=OUT[g.par][:, t, :], in0=e2[:, t, :],
                                                   scalar=coef[g.par][:, t, 2:3], in1=OUT[g.par][:, t, :],
                                                   op0=ALU.mult, op1=ALU.add)
                ins.then_inc(out_ready, 1)

            def expert0(g):
                dve.wait_ge(ex_taken, g.count(E, 1))
                mix(g, 2, 0)

            def turn(g, first, last):
                def unit(name):
                    dve.wait_ge(unit_ready, g.count(NU, UNITS.index(name) + 1))
                    return S[g.bank(name)], released[g.bank(name)]

                for t in range(NT):
                    dve.wait_ge(z_taken, g.count(NT, t + 1))
                    dve.tensor_tensor(pl[:, t, :], S[g.bank(f"tok{t}")][:, P:TOKW], tokb[:, :], ALU.add) \
                        .then_inc(released[g.bank(f"tok{t}")], 1)
                for t in range(NT):
                    b = g.bank(f"tok{t}")
                    dve.wait_ge(released[b], g.uses_before(f"tok{t}") + 1)
                    dve.bn_stats(stats["c"][:, t, :], pl[:, t, 0:P])
                dve.drain()
                for t in range(NT):
                    ins = dve.bn_aggr(mv["c"][:, t, :], stats["c"][:, t, :])
                ins.then_inc(c_stats, 1)
                if not last:
                    x_moments(g.next())
                if not first:
                    expert0(g.prev())

                def silu(j):
                    dve.wait_ge(th_ready, g.count(4, j + 1))
                    a, a_free = S[g.bank(f"a{j}")], released[g.bank(f"a{j}")]
                    dve.scalar_tensor_tensor(out=gate[:, j, :], in0=th[:, j, :], scalar=1.0, in1=a[:, :],
                                             op0=ALU.add, op1=ALU.mult).then_inc(a_free, 1)
                    b, b_free = unit(f"b{j}")
                    dve.wait_ge(a_free, g.uses_before(f"a{j}") + 1)
                    dve.tensor_tensor(hid[0][:, j, :], gate[:, j, :], b[:, :], ALU.mult).then_inc(b_free, 1)

                dve.wait_ge(qk_high, g.count(1, 1))
                qk = S[g.bank("qk")]
                dve.tensor_tensor(Q[C:2 * C, :], qk[C:2 * C, :], Q[C:2 * C, :], ALU.subtract).then_inc(qk_split, 1)
                dve.tensor_tensor(K[2 * C:3 * C, :], qk[3 * C:4 * C, :], K[2 * C:3 * C, :], ALU.subtract) \
                    .then_inc(released[g.bank("qk")], 1)
                silu(0)

                rs = [0]

                def route(ins):
                    rs[0] += 1
                    ins.then_inc(route_step, 1)
                    dve.wait_ge(route_step, g.count(ROUTE_STEPS, rs[0]))

                logit = pl[:, :, P:P + E]
                mine = logit.unsqueeze(3).broadcast_to([P, NT, E, E])
                other = logit.unsqueeze(2).broadcast_to([P, NT, E, E])
                route(dve.tensor_tensor(same[:, :, :, :], other, mine, ALU.is_equal))
                route(dve.tensor_tensor(same[:, :, :, :], same[:, :, :, :],
                                        earlier[:, :, :].unsqueeze(1).broadcast_to([P, NT, E, E]), ALU.mult))
                route(dve.tensor_tensor(more[:, :, :, :], other, mine, ALU.is_gt))
                route(dve.tensor_tensor(more[:, :, :, :], more[:, :, :, :], same[:, :, :, :], ALU.add))
                route(dve.tensor_reduce(rank[:, :, :], more[:, :, :, :], AX.X, ALU.add))
                route(dve.scalar_tensor_tensor(out=top[:, :, :], in0=rank[:, :, :], scalar=1.5, in1=logit,
                                               op0=ALU.is_lt, op1=ALU.mult))
                route(dve.tensor_reduce(topsum[:, :], top[:, :, :], AX.X, ALU.add))
                dve.scalar_tensor_tensor(out=lean[:, :, :], in0=topsum[:, :].unsqueeze(2).broadcast_to([P, NT, E]),
                                         scalar=-0.5, in1=logit, op0=ALU.mult, op1=ALU.add).then_inc(lean_ready, 1)
                route(dve.tensor_scalar(half[:, :, :], rank[:, :, :], 1.5, 0.5, ALU.is_lt, ALU.mult))

                for s in range(NT):
                    n = (s + 1) * P
                    sc, free = unit(f"sc{s}")
                    dve.tensor_tensor(pr[:, s, 0:n], sc[:, 0:n], mask[:, T - n:T], ALU.mult).then_inc(free, 1)
                dve.wait_ge(h2_high, g.count(1, 1))
                dve.tensor_tensor(h2l[:, :], h2[:, :], h2h[:, :], ALU.subtract).then_inc(h2_low, 1)
                silu(1)
                dve.wait_ge(tlean_ready, g.count(1, 1))
                route(dve.scalar_tensor_tensor(out=coef[g.par][:, :, :], in0=tlean[:, :, :], scalar=1.0,
                                               in1=half[:, :, :], op0=ALU.add, op1=ALU.mult))
                assert rs[0] == ROUTE_STEPS
                if not first:
                    expert2_scale(g.prev())
                    expert1(g.prev())
                wait(dve, out_stored[g.par], g.half(DMA_INC, 0))
                dve.wait_ge(att_ready, g.count(1, 1))
                dve.tensor_tensor(OUT[g.par][:, :, :], ATT[:, :, :], X[g.par][:, :, :], ALU.add) \
                    .then_inc(att_added, 1)
                silu(2)
                silu(3)
                if not first:
                    expert2_add(g.prev())
                f2, free = unit("f2")
                dve.scalar_tensor_tensor(out=u[:, :], in0=f2[:, :], scalar=vec("f2b"), in1=h2[:, :],
                                         op0=ALU.add, op1=ALU.add).then_inc(free, 1)
                dve.wait_ge(att_added, g.count(1, 1))
                if not last:
                    x_low(g.next())
                mix(g, 1, 3)
                dve.wait_ge(u_turned, g.count(1, 1))
                for t in range(NT):
                    dve.bn_stats(stats["u"][:, t, :], TR[:, t * P:(t + 1) * P])
                dve.drain()
                for t in range(NT):
                    ins = dve.bn_aggr(mv["u"][:, t, :], stats["u"][:, t, :])
                ins.then_inc(u_stats, 1)

            def tail(g):
                expert0(g)
                expert2_scale(g)
                expert1(g)
                expert2_add(g)

            turns(dve, turn, tail)

        @block.tensor
        def _(pe):
            done = [0]

            def setup(name, n_out, lhsT, rhs, rows_=P):
                assert MM[done[0]] == name
                if done[0] >= len(ALL):
                    pe.wait_ge(setup_took, done[0] - len(ALL) + 1)
                pe.matmul(prod(name, rows_, n_out), lhsT, rhs, start=True, stop=True).then_inc(setup_mm, 1)
                done[0] += 1

            def after(name):
                pe.wait_ge(setup_took, MM.index(name) + 1)

            pe.wait_ge(w_loaded[0], DMA_INC)
            setup("qk", 4 * C, w("basisT"), w("qkT"))
            setup("vT", P, w("vcT"), w("basisT"), C)
            setup("ce1", P + 1, w("ce_wv"), w("ce_x0"))
            setup("oT", P, w("ocT"), w("basisT"), C)
            pe.wait_ge(w_loaded[2], DMA_INC)
            setup("me1", P + 1, w("me_wv"), w("me_x0"))
            after("ce1")
            setup("ce2", P + 1, w("ce_wo"), ce_x1[:, :])
            after("oT")
            setup("vo", P, vT[:, :], oT[:, :])

            def turn_x(g):
                for t in range(NT):
                    pe.wait_ge(x_normed, g.count(NT, t + 1))
                    ins = pe.transpose(TR[:, t * P:(t + 1) * P], xn[:, t, :], ident[:, :])
                ins.then_inc(x_turned, 1)

            pe.wait_ge(pool_const, POOL_CONSTS)
            turn_x(Group(0, 0))
            after("me1")
            setup("me2", P + 1, w("me_wo"), me_x1[:, :])
            after("ce2")
            setup("ce", P, ce_x2[:, 0:P], ident[:, :])
            pe.wait_ge(setup_dve, CE_BIAS_LINK)
            setup("ce_b", P, bcast[:, 0, :], ident[:, :])
            after("me2")
            setup("me", 2 * P, me_x2[:, 0:P], w("me_c1w"))
            pe.wait_ge(setup_took, MM.index("me_b") - len(ALL) + 1)
            for j in range(2):
                ins = pe.matmul(flat[MM.index("me_b") % len(ALL)][:, j:j + 1], w("me_c1w", j * P, P),
                                me_x2[:, P:P + 1], start=True, stop=True)
            ins.then_inc(setup_mm, 1)
            done[0] += 1
            setup("gen", P, center[:, :], gen_s[:, :])
            setup("gen_b", P, bcast[:, 1, :], w("gen_w"))

            after("gen_b")
            pe.wait_ge(setup_done, 1)
            pe.wait_ge(split_low, 2)

            def expert_sum(g, e, parts, col):
                bank = EX[EX_BANK[e]][:, :, :].rearrange("p t n -> p (t n)")
                for j in range(parts):
                    pe.wait_ge(hid_low[e], g.count(parts, j + 1))
                    wh, wl = WH[:, col + j * P:col + (j + 1) * P], WL[:, col + j * P:col + (j + 1) * P]
                    pe.matmul(bank, wh, hidh[e][:, j, :], start=(j == 0), stop=False)
                    pe.matmul(bank, wh, hidl[e][:, j, :], start=False, stop=False)
                    ins = pe.matmul(bank, wl, hidh[e][:, j, :], start=False, stop=(j == parts - 1))
                ins.then_inc(ex_summed, 1)

            def expert2(g):
                pe.wait_ge(ex_taken, g.count(E, 2))
                for t in range(NT):
                    ins = pe.matmul(EX[EX_BANK[2]][:, t, :], u[:, t * P:(t + 1) * P], gen_c[:, :],
                                    start=True, stop=True)
                ins.then_inc(ex_ready, 1)

            def expert_turn(g, n, e):
                pe.wait_ge(ex_copied, g.count(3, n))
                for t in range(NT):
                    ins = pe.transpose(EX[EX_BANK[e]][:, t, :], exT[:, t * P:(t + 1) * P], ident[:, :])
                ins.then_inc(ex_ready, 1)

            def turn(g, first, last):
                def fill(name):
                    wait(pe, released[g.bank(name)], g.uses_before(name))
                    return S[g.bank(name)]

                def three(name, col, hi, lo):
                    bank = fill(name)
                    wh, wl = WH[:, col:col + P], WL[:, col:col + P]
                    pe.matmul(bank[:, :], wh, hi, start=True, stop=False)
                    pe.matmul(bank[:, :], wh, lo, start=False, stop=False)
                    pe.matmul(bank[:, :], wl, hi, start=False, stop=True).then_inc(unit_ready, 1)

                h, l, full = xh[g.par][:, :], xl[g.par][:, :], xT[g.par]

                pe.wait_ge(x_split, g.count(1, 1))
                for t in range(NT):
                    bank = fill(f"tok{t}")
                    pe.matmul(bank[:, 0:TOKW], full[:, t * P:(t + 1) * P], tokw[:, :], start=True, stop=True) \
                        .then_inc(unit_ready, 1)
                three("qk", SPLIT["qk"], h, l)
                if not first:
                    pe.wait_ge(ex_taken, g.prev().count(E, 1))
                    expert_sum(g.prev(), 1, 2, SPLIT["me2"])

                def gates(j):
                    three(f"a{j}", SPLIT["w1"] + j * P, h, l)
                    three(f"b{j}", SPLIT["w3"] + j * P, h, l)

                gates(0)
                if not first:
                    expert2(g.prev())
                    expert_turn(g.prev(), 3, 1)
                for j in range(4):
                    three(f"c{j}", SPLIT["ml"] + j * P, h, l)
                wait(pe, u_stats, g.count(1, 0))
                for t in range(NT):
                    pe.wait_ge(c_normed, g.count(NT, t + 1))
                    ins = pe.transpose(TR[:, t * P:(t + 1) * P], n1[:, t, :], ident[:, :])
                ins.then_inc(c_turned, 1)

                pe.wait_ge(qk_split, g.count(1, 1))
                for s in range(NT):
                    bank = fill(f"sc{s}")
                    if s == 0:
                        b = g.bank("qk")
                        pe.wait_ge(released[b], g.uses_before("qk") + 1)
                    pe.matmul(bank[:, 0:(s + 1) * P], K[:, s * P:(s + 1) * P], Q[:, 0:(s + 1) * P],
                              start=True, stop=True).then_inc(unit_ready, 1)
                gates(1)
                pe.wait_ge(h2_low, g.count(1, 1))
                three("f1_0", SPLIT["f1"], h2h[:, :], h2l[:, :])
                three("f1_1", SPLIT["f1"] + P, h2h[:, :], h2l[:, :])
                wait(pe, att_added, g.count(1, 0))
                b = g.bank(f"sc{NT - 1}")
                pe.wait_ge(released[b], g.uses_before(f"sc{NT - 1}") + 1)
                for t in range(NT):
                    for s in range(t, NT):
                        ins = pe.matmul(ATT[:, t, :], pr[:, s, t * P:(t + 1) * P], z[:, s, :],
                                        start=(s == t), stop=(s == NT - 1))
                ins.then_inc(att_ready, 1)
                gates(2)
                gates(3)
                if first:
                    pe.wait_ge(split_low, len(WEIGHT_SPLITS))
                else:
                    pe.wait_ge(ex_taken, g.prev().count(E, 4))
                expert_sum(g, 3, 4, SPLIT["ml2"])
                bank = fill("f2")
                for j in range(2):
                    pe.wait_ge(hid_low[2], g.count(2, j + 1))
                    wh, wl = (m[:, SPLIT["f2"] + j * P:SPLIT["f2"] + (j + 1) * P] for m in (WH, WL))
                    pe.matmul(bank[:, :], wh, hidh[2][:, j, :], start=(j == 0), stop=False)
                    pe.matmul(bank[:, :], wh, hidl[2][:, j, :], start=False, stop=False)
                    ins = pe.matmul(bank[:, :], wl, hidh[2][:, j, :], start=False, stop=(j == 1))
                ins.then_inc(unit_ready, 1)
                pe.wait_ge(h2_ready, g.count(1, 1))
                if not last:
                    turn_x(g.next())
                expert_turn(g, 1, 3)
                if not first:
                    pe.wait_ge(ex_taken, g.prev().count(E, 3))
                expert_sum(g, 0, 4, SPLIT["sw2"])
                three("m0", SPLIT["me"], h, l)
                three("m1", SPLIT["me"] + P, h, l)
                expert_turn(g, 2, 0)
                if not last:
                    pe.wait_ge(x_split, g.next().count(1, 1))
                b = g.bank("f2")
                pe.wait_ge(released[b], g.uses_before("f2") + 1)
                for t in range(NT):
                    ins = pe.transpose(TR[:, t * P:(t + 1) * P], u[:, t * P:(t + 1) * P], ident[:, :])
                ins.then_inc(u_turned, 1)

            def tail(g):
                pe.wait_ge(ex_taken, g.count(E, 1))
                expert_sum(g, 1, 2, SPLIT["me2"])
                expert2(g)
                expert_turn(g, 3, 1)

            turns(pe, turn, tail)


ROUTE_STEPS = 9
DECAY_STEPS = ([("power", 0), ("power", 1), ("times", 0), ("power", 2), ("take", 0)]
               + [s for n in range(1, 7) for s in (("power", n + 2), ("times", n), ("take", n))])
POOL_CONSTS = 10
CE_BIAS_LINK = 6


def kernel(**inputs):
    import numpy as np
    import concourse.bacc as bacc
    from concourse.bass_utils import run_bass_kernel_spmd

    a = {k[7:] if k.startswith("L0_ffn_") else k: np.asarray(v) for k, v in inputs.items()}

    def chunks(m):
        return np.concatenate([m[j * P:(j + 1) * P] for j in range(m.shape[0] // P)], axis=1)

    basis_t = a["L0_attn_basis"].T
    q, k = a["L0_attn_q_coeffs"].T, a["L0_attn_k_coeffs"].T
    packed = {
        "basisT": basis_t, "qkT": np.concatenate([q, q, k, k], axis=1),
        "vcT": a["L0_attn_v_coeffs"].T, "ocT": a["L0_attn_o_coeffs"].T,
        "ce_x0": np.concatenate([a["ce_syn_w"].T, a["ce_syn_b"][:, None]], axis=1),
        "ce_wv": a["ce_wv"], "ce_wo": a["ce_wo"], "router": a["router_w"], "gen_w": a["ce_gen_w"],
        "sw_w1": a["sw_w1"], "sw_w3": a["sw_w3"],
        "me_x0": np.concatenate([a["me_eq_w"].T, a["me_eq_b"][:, None]], axis=1),
        "me_wv": a["me_wv"], "me_wo": a["me_wo"], "me_c1w": a["me_c1w"],
        "ml_w1": a["ml_w1"], "f1w": a["ce_f1w"],
        "f2w": chunks(a["ce_f2w"]), "sw_w2": chunks(a["sw_w2"]), "me_c2w": chunks(a["me_c2w"]),
        "ml_w2": chunks(a["ml_w2"]),
    }
    weights = np.concatenate([packed[name] for load in LOADS for name, _ in load], axis=1)
    c1b, f1b, mlb = (a[n].reshape(-1, P) for n in ("me_c1b", "ce_f1b", "ml_b1"))
    vecs = {"me_bv": a["me_bv"], "me_bo": a["me_bo"], "me_c1b0": c1b[0], "me_c1b1": c1b[1],
            "ce_bv": a["ce_bv"], "ce_bo": a["ce_bo"], "n1g": a["ce_n1g"], "n1b": a["ce_n1b"],
            "f1b0": f1b[0], "f1b1": f1b[1], "f2b": a["ce_f2b"], "n2g": a["ce_n2g"], "n2b": a["ce_n2b"],
            "ml_b10": mlb[0], "ml_b11": mlb[1], "ml_b12": mlb[2], "ml_b13": mlb[3],
            "me_c2b": a["me_c2b"], "ml_b2": a["ml_b2"]}
    row = np.concatenate([a["ce_gen_b"], a["router_b"], a["load_balancer"],
                          a["L0_attn_decay_logit"].reshape(1), a["L0_attn_out_scale"].reshape(1)])
    arrays = {
        "x": np.ascontiguousarray(a["L0_attn_x"]),
        "weights": np.ascontiguousarray(weights),
        "vecs": np.ascontiguousarray(np.stack([vecs[n] for n in VECS], axis=1)),
        "rows": np.ascontiguousarray(row[None, :]),
    }
    nc = bacc.Bacc("TRN2", target_bir_lowering=False, num_devices=1)
    args = [nc.dram_tensor(n, v.shape, mybir.dt.from_np(v.dtype), kind="ExternalInput").ap()
            for n, v in arrays.items()]
    out = nc.dram_tensor("out", (GROUPS, T, P), F32, kind="ExternalOutput").ap()
    build(nc, *args, out)
    r = run_bass_kernel_spmd(nc, [arrays], core_ids=[0])
    return r.results[0]["out"]
```

```python
from contextlib import ExitStack

import concourse.bass as bass
from concourse import mybir

F32 = mybir.dt.float32
F32R = mybir.dt.float32r
I32 = mybir.dt.int32
ALU = mybir.AluOpType
ACT = mybir.ActivationFunctionType
AX = mybir.AxisListType

P = 128
GROUPS = 16
T = 512
NT = T // P
PAIRS = GROUPS // 2
C = 32
E = 4
I = 512
EPS = 1e-5
DMA_INC = 16

LOADS = [
    [("basisT", P), ("qkT", 4 * C), ("vcT", C), ("ocT", C), ("ce_x0", P + 1), ("ce_wv", P), ("ce_wo", P),
     ("router", E), ("gen_w", P)],
    [("sw_w1", I), ("sw_w3", I)],
    [("ml_w1", I), ("f1w", 2 * P)],
    [("me_x0", P + 1), ("me_wv", P), ("me_wo", P), ("me_c1w", 2 * P)],
    [("f2w", 2 * P), ("sw_w2", I), ("me_c2w", 2 * P), ("ml_w2", I)],
]
COL, LOAD_OF, SPAN = {}, {}, []
_at = 0
for _n, _load in enumerate(LOADS):
    _first = _at
    for _name, _width in _load:
        COL[_name] = (_at, _width)
        LOAD_OF[_name] = _n
        _at += _width
    SPAN.append((_first, _at))
WCOLS = _at

VECS = ["me_bv", "me_bo", "me_c1b0", "me_c1b1", "ce_bv", "ce_bo", "n1g", "n1b", "f1b0", "f1b1", "f2b",
        "n2g", "n2b", "ml_b10", "ml_b11", "ml_b12", "ml_b13", "ml_b2"]
ROWS = {"gen_b": (0, P), "router_b": (P, E), "balancer": (P + E, E), "decay_logit": (P + 2 * E, 1),
        "out_scale": (P + 2 * E + 1, 1), "me_c2b": (P + 2 * E + 2, P)}
RCOLS = 2 * (P + E + 1)

SPLIT, _at = {}, 0
for _name, _width in (("w1", I), ("w3", I), ("ml", I), ("f1", 2 * P), ("f2", 2 * P), ("sw2", I),
                      ("ml2", I), ("me", 2 * P), ("qk", 4 * C)):
    SPLIT[_name] = _at
    _at += _width
SCOLS = _at
WEIGHT_SPLITS = [(SPLIT["w1"], "sw_w1", 2 * I), (SPLIT["ml"], "ml_w1", I + 2 * P), (SPLIT["f2"], "f2w", 2 * P),
                 (SPLIT["sw2"], "sw_w2", I), (SPLIT["ml2"], "ml_w2", I)]
FIRST_SPLITS = 2
EX_BANK = {3: 0, 0: 1, 2: 1, 1: 0}

TOKW = 2 * P + E

UNITS = ([f"tok{t}" for t in range(NT)] + ["a0", "b0", "c0", "c1", "c2", "c3"]
         + [f"sc{t}" for t in range(NT)] + ["a1", "b1", "f1_0", "f1_1", "a2", "b2", "a3", "b3", "f2", "m0", "m1", "ut"])
NU = len(UNITS)
BANKS = 4
assert 2 * NU % BANKS == 0


class Group:

    def __init__(self, pair, off):
        self.pair, self.off = pair, off
        self.par = off % 2

    def next(self):
        return Group(self.pair, self.off + 1)

    def prev(self):
        return Group(self.pair, self.off - 1)

    def count(self, per, n):
        return self.pair * (2 * per) + (self.off * per + n)

    def half(self, per, n):
        return self.pair * per + (self.off // 2 * per + n)

    def index(self):
        return self.pair * 2 + self.off

    def bank(self, unit):
        return (NU * self.off + UNITS.index(unit)) % BANKS

    def uses_before(self, unit):
        return self.pair * (2 * NU // BANKS) + (NU * self.off + UNITS.index(unit)) // BANKS


def two_more(g):
    return not (isinstance(g.pair, int) and g.pair == PAIRS - 1)


def wait(eng, sem, value):
    if not isinstance(value, int) or value > 0:
        eng.wait_ge(sem, value)


def build(nc: bass.Bass, x: bass.AP, weights: bass.AP, vecs: bass.AP, rows: bass.AP, out: bass.AP):
    with ExitStack() as ctx:
        def sb(name, shape, dt=F32):
            return ctx.enter_context(nc.sbuf_tensor(name, shape, dt))

        def sem(name):
            return ctx.enter_context(nc.semaphore(name))

        W = sb("W", [P, WCOLS])
        VEC = sb("VEC", [P, len(VECS)])
        ROW = sb("ROW", [P, RCOLS])
        WH = sb("WH", [P, SCOLS], F32R)
        WL = sb("WL", [P, SCOLS], F32R)
        tokw = sb("tokw", [P, TOKW])
        tokb = sb("tokb", [P, P + E])
        ident = sb("ident", [P, P])
        center = sb("center", [P, P])
        me_b = sb("me_b", [P, 2])
        gen_c = sb("gen_c", [P, P])
        gen_bias = sb("gen_bias", [P, P])
        earlier = sb("earlier", [P, E, E])
        minus1 = sb("minus1", [P, NT])
        eps4 = sb("eps4", [P, NT])
        nhalf = sb("nhalf", [P, NT])
        mask = sb("mask", [P, T])
        scaled = sb("scaled", [P, I])
        table_pick = sb("table_pick", [P, 1])
        power = sb("power", [P, 9])

        X = [sb(f"X{k}", [P, NT, P]) for k in range(2)]
        OUT = [sb(f"OUT{k}", [P, NT, P]) for k in range(2)]
        xn = sb("xn", [P, NT, P])
        xT = [sb(f"xT{k}", [P, T]) for k in range(2)]
        xh = [sb(f"xh{k}", [P, T], F32R) for k in range(2)]
        xl = [sb(f"xl{k}", [P, T], F32R) for k in range(2)]
        z = sb("z", [P, NT, P])
        pl = sb("pl", [P, NT, P + E])
        n1 = sb("n1", [P, NT, P])
        Q = sb("Q", [3 * C, T], F32R)
        K = sb("K", [3 * C, T], F32R)
        th = sb("th", [P, NT, T])
        hid = {e: sb(f"hid{e}", [P, k, T]) for e, k in ((0, 4), (3, 4), (1, 2), (2, 2))}
        hidh, hidl = ({e: sb(f"{n}{e}", [P, k, T], F32R) for e, k in ((0, 4), (3, 4), (2, 2))}
                      for n in ("hidh", "hidl"))
        exT = sb("exT", [P, T])
        h2 = sb("h2", [P, T])
        h2h = sb("h2h", [P, T], F32R)
        h2l = sb("h2l", [P, T], F32R)
        u = sb("u", [P, T])
        stats = {k: sb(f"stats_{k}", [P, NT, 6]) for k in "xcu"}
        mv = {k: sb(f"mv_{k}", [P, NT, 2]) for k in "xcu"}
        negmean = {k: sb(f"negmean_{k}", [P, NT]) for k in "xc"}
        veps = {k: sb(f"veps_{k}", [P, NT]) for k in "xcu"}
        rstd = {k: sb(f"rstd_{k}", [P, NT]) for k in "xcu"}
        more = sb("more", [P, NT, E, E])
        same = sb("same", [P, NT, E, E])
        rank = sb("rank", [P, NT, E])
        top = sb("top", [P, NT, E])
        topsum = sb("topsum", [P, NT])
        lean = sb("lean", [P, NT, E])
        tlean = sb("tlean", [P, NT, E])
        half = sb("half", [P, NT, E])
        coef = [sb(f"coef{k}", [P, NT, E]) for k in range(2)]

        vT = sb("vT", [C, P])
        oT = sb("oT", [C, P])
        ce_x1, ce_x2, me_x1, me_x2 = (sb(name, [P, P + 1]) for name in ("ce_x1", "ce_x2", "me_x1", "me_x2"))
        gen_s = sb("gen_s", [P, P])
        bcast = sb("bcast", [P, 2, P])
        PW = 2 * P + 1
        with ExitStack() as lent:
            bit, expo, pacc, ptry = (lent.enter_context(nc.sbuf_tensor(name, shape, dt)) for name, shape, dt in (
                ("bit", [P, 7, PW], I32), ("expo", [P, PW], I32), ("pacc", [P, PW], F32), ("ptry", [P, PW], F32)))
        pr = sb("pr", [P, NT, T])
        e2 = sb("e2", [P, NT, P])
        sb("rest_of_powers", [P, 10 * PW - 5 * T + 4 * 8])
        gate = sb("gate", [P, 4, T])

        S = [ctx.enter_context(nc.psum_tensor(f"S{b}", [P, T], F32)) for b in range(BANKS)]
        TR = ctx.enter_context(nc.psum_tensor("TR", [P, T], F32))
        EX = [ctx.enter_context(nc.psum_tensor(f"EX{b}", [P, NT, P], F32)) for b in range(2)]
        ATT = ctx.enter_context(nc.psum_tensor("ATT", [P, NT, P], F32))

        qk_bank = ATT[:, :, :].rearrange("p t n -> p (t n)")

        w_loaded = [sem(f"w_loaded{n}") for n in range(len(LOADS))]
        vec_loaded = sem("vec_loaded")
        row_loaded = sem("row_loaded")
        x_loaded = [sem(f"x_loaded{k}") for k in range(2)]
        out_stored = [sem(f"out_stored{k}") for k in range(2)]
        pool_const = sem("pool_const")
        expo_ready = sem("expo_ready")
        decay_tanh = sem("decay_tanh")
        setup_mm = sem("setup_mm")
        setup_took = sem("setup_took")
        setup_dve = sem("setup_dve")
        setup_act = sem("setup_act")
        split_high = sem("split_high")
        half_done = sem("half_done")
        split_low = sem("split_low")
        decay_step = sem("decay_step")
        unit_ready = sem("unit_ready")
        released = [sem(f"released{b}") for b in range(BANKS)]
        x_stats = sem("x_stats")
        x_normed = sem("x_normed")
        x_turned = sem("x_turned")
        x_high = sem("x_high")
        x_split = sem("x_split")
        qk_ready = sem("qk_ready")
        qk_high = sem("qk_high")
        qk_split = sem("qk_split")
        z_taken = sem("z_taken")
        c_stats = sem("c_stats")
        c_normed = sem("c_normed")
        c_turned = sem("c_turned")
        h2_ready = sem("h2_ready")
        h2_high = sem("h2_high")
        h2_low = sem("h2_low")
        lean_ready = sem("lean_ready")
        tlean_ready = sem("tlean_ready")
        th_ready = sem("th_ready")
        att_ready = sem("att_ready")
        att_added = sem("att_added")
        hid_high = {e: sem(f"hid_high{e}") for e in (0, 2, 3)}
        hid_low = {e: sem(f"hid_low{e}") for e in (0, 2, 3)}
        ex_summed = sem("ex_summed")
        ex_copied = sem("ex_copied")
        u_stats = sem("u_stats")
        u_rstd = sem("u_rstd")
        ex_ready = sem("ex_ready")
        ex_taken = sem("ex_taken")
        bias1_added = sem("bias1_added")
        route_step = sem("route_step")
        out_ready = sem("out_ready")

        def w(name, first=0, width=None):
            at, full = COL[name]
            return W[:, at + first:at + first + (full if width is None else width)]

        def vec(name):
            n = VECS.index(name)
            return VEC[:, n:n + 1]

        def row(name):
            at, width = ROWS[name]
            return ROW[:, at:at + width]

        ALL = [S[0], S[1], S[2], S[3], EX[0], EX[1], ATT]
        flat = [b[:, :] if len(b.shape) == 2 else b[:, :, :].rearrange("p t n -> p (t n)") for b in ALL]
        FIRST = ["ce1", "vT", "oT", "qk", "ce2", "vo", "ce", "ce_b"]
        MM = FIRST + ["me1", "gen", "me2", "gen_b", "me", "me_b"]
        TAKEN = [name for name in MM if name not in ("vT", "oT")]
        bank_of = [n % len(ALL) if n < len(FIRST) else ALL.index(EX[n % 2]) for n in range(len(MM))]

        def prod(name, rows_=P, cols=P):
            return flat[bank_of[MM.index(name)]][0:rows_, 0:cols]

        block = ctx.enter_context(nc.Block())

        def turns(eng, turn, tail):
            turn(Group(0, 0), True, False)
            turn(Group(0, 1), False, False)
            with eng.Fori(1, PAIRS - 1) as i:
                turn(Group(i, 0), False, False)
                turn(Group(i, 1), False, False)
            turn(Group(PAIRS - 1, 0), False, False)
            turn(Group(PAIRS - 1, 1), False, True)
            tail(Group(PAIRS - 1, 1))

        @block.sync
        def _(sp):
            def load_x(g):
                sp.dma_start(X[g.par][:, :, :], x[g.index()].rearrange("(t p) h -> p t h", p=P)) \
                    .then_inc(x_loaded[g.par], DMA_INC)

            load_x(Group(0, 0))
            for n, (a, b) in enumerate(SPAN):
                sp.dma_start(W[:, a:b], weights[:, a:b]).then_inc(w_loaded[n], DMA_INC)
            load_x(Group(0, 1))

            def store(g):
                sp.wait_ge(out_ready, g.count(1, 1))
                sp.dma_start(out[g.index()].rearrange("(t p) h -> p t h", p=P), OUT[g.par][:, :, :]) \
                    .then_inc(out_stored[g.par], DMA_INC)

            def turn(g, first, last):
                if not first:
                    store(g.prev())
                if two_more(g):
                    sp.wait_ge(att_added, g.count(1, 1))
                    load_x(Group(g.pair, g.off + 2))

            turns(sp, turn, store)
            for k in range(2):
                sp.wait_ge(out_stored[k], DMA_INC * PAIRS)

        @block.gpsimd
        def _(pool):
            steps = [0]

            def const(ins):
                steps[0] += 1
                ins.then_inc(pool_const, 1)
                pool.wait_ge(pool_const, steps[0])

            pool.iota(expo[:, 0:P], [[-1, P]], base=-1, channel_multiplier=1).then_inc(expo_ready, 1)
            pool.iota(expo[:, P:P + 1], [[0, 1]], base=0, channel_multiplier=1).then_inc(expo_ready, 1)
            pool.iota(expo[:, P + 1:PW], [[-1, P]], base=P - 1, channel_multiplier=0).then_inc(expo_ready, 1)
            const(pool.memset(nhalf[:, :], -0.5))
            const(pool.memset(minus1[:, :], -1.0))
            const(pool.memset(eps4[:, :], EPS))
            const(pool.memset(ident[:, :], 0.0))
            const(pool.affine_select(out=ident[:, :], in_=ident[:, :], compare_op=ALU.not_equal, fill=1.0, base=0,
                                     pattern=[[-1, P]], channel_multiplier=1))
            const(pool.tensor_scalar(center[:, :], ident[:, :], 1.0, -1.0 / P, ALU.mult, ALU.add))
            const(pool.memset(earlier[:, :, :], 0.0))
            for e in range(1, E):
                const(pool.memset(earlier[:, e, 0:e], 1.0))

            def root(k):
                pool.tensor_tensor(veps[k][:, :], mv[k][:, :, 1], eps4[:, :], ALU.add)
                pool.drain()
                return pool.tensor_tensor(rstd[k][:, :], veps[k][:, :], nhalf[:, :], ALU.pow)

            def norm(k, src, dst, done):
                root(k)
                pool.tensor_tensor(negmean[k][:, :], mv[k][:, :, 0], minus1[:, :], ALU.mult)
                pool.drain()
                for t in range(NT):
                    pool.tensor_scalar(dst[:, t, :], src[:, t, 0:P], negmean[k][:, t:t + 1], rstd[k][:, t:t + 1],
                                       ALU.add, ALU.mult).then_inc(done, 1)

            def norm_x(g):
                pool.wait_ge(x_stats, g.count(1, 1))
                norm("x", X[g.par], xn, x_normed)

            norm_x(Group(0, 0))

            def low_weights(splits):
                for n in splits:
                    first_col, name, width = WEIGHT_SPLITS[n]
                    pool.wait_ge(split_high, n + 1)
                    src = scaled[:, :] if name == "sw_w2" else w(name, 0, width)
                    cols = slice(first_col, first_col + width)
                    pool.tensor_tensor(WL[:, cols], src, WH[:, cols], ALU.subtract).then_inc(split_low, 1)

            low_weights(range(FIRST_SPLITS))

            def turn(g, first, last):
                def low(e, a, b):
                    parts = {3: 2, 2: 1, 0: 3}[e]
                    part = {3: {0: 1, 2: 2}, 0: {0: 1, 2: 2, 3: 3}}.get(e, {0: 1})[a]
                    pool.wait_ge(hid_high[e], g.count(parts, part))
                    for j in range(a, b):
                        pool.tensor_tensor(hidl[e][:, j, :], hid[e][:, j, :], hidh[e][:, j, :], ALU.subtract) \
                            .then_inc(hid_low[e], 1)

                pool.wait_ge(c_stats, g.count(1, 1))
                norm("c", pl, n1, c_normed)
                if not first:
                    root_u(g.prev())
                if first:
                    low_weights(range(FIRST_SPLITS, len(WEIGHT_SPLITS)))
                    norm_x(g.next())
                low(3, 0, 2)
                low(3, 2, 4)
                low(2, 0, 2)
                low(0, 0, 2)
                low(0, 2, 3)
                low(0, 3, 4)
                if two_more(g):
                    norm_x(Group(g.pair, g.off + 2))

            def root_u(g):
                pool.wait_ge(u_stats, g.count(1, 1))
                root("u").then_inc(u_rstd, 1)

            turns(pool, turn, root_u)

        @block.scalar
        def _(act):
            act.dma_start(ROW[:, :], rows[0:1, :].broadcast_to([P, RCOLS])).then_inc(row_loaded, DMA_INC)
            act.dma_start(VEC[:, :], vecs).then_inc(vec_loaded, DMA_INC)
            act.wait_ge(row_loaded, DMA_INC)
            act.activation(table_pick[:, :], row("decay_logit"), ACT.Gelu)
            act.activation(power[:, 8:9], row("decay_logit"), ACT.Tanh, scale=0.5).then_inc(decay_tanh, 1)

            def take_x(g):
                act.wait_ge(x_turned, g.count(1, 1))
                act.copy(xT[g.par][:, :], TR[:, :])
                act.copy(xh[g.par][:, :], TR[:, :]).then_inc(x_high, 1)

            def high_weights(n):
                first_col, name, width = WEIGHT_SPLITS[n]
                act.wait_ge(w_loaded[LOAD_OF[name]], DMA_INC)
                src = w(name, 0, width)
                if name == "sw_w2":
                    act.mul(scaled[:, :], src, 0.5).then_inc(half_done, 1)
                    act.wait_ge(half_done, 1)
                    src = scaled[:, :]
                act.copy(WH[:, first_col:first_col + width], src).then_inc(split_high, 1)

            act.wait_ge(setup_mm, MM.index("vT") + 1)
            act.copy(vT[:, :], prod("vT", C)).then_inc(setup_act, 1)
            act.wait_ge(setup_mm, MM.index("oT") + 1)
            act.mul(oT[:, :], prod("oT", C), row("out_scale")[0:C]).then_inc(setup_act, 1)
            act.copy(tokw[:, 2 * P:TOKW], w("router")).then_inc(setup_act, 1)
            high_weights(0)
            act.wait_ge(vec_loaded, DMA_INC)
            act.mul(gen_s[:, :], w("gen_w"), vec("n2g")).then_inc(setup_act, 1)
            act.copy(bcast[:, 1, :], vec("n2b").broadcast_to([P, P])).then_inc(setup_act, 1)
            take_x(Group(0, 0))
            high_weights(1)

            def expert_copy(g, n, e, bias):
                act.wait_ge(ex_summed, g.count(2, n))
                src = EX[EX_BANK[e]][:, :, :].rearrange("p t n -> p (t n)")
                if bias is None:
                    ins = act.copy(exT[:, :], src)
                else:
                    ins = act.activation(exT[:, :], src, ACT.Identity, bias=vec(bias))
                ins.then_inc(ex_copied, 1)

            def turn(g, first, last):
                def unit(name):
                    act.wait_ge(unit_ready, g.count(NU, UNITS.index(name) + 1))
                    return S[g.bank(name)], released[g.bank(name)]

                for t in range(NT):
                    tok, _ = unit(f"tok{t}")
                    act.copy(z[:, t, :], tok[:, 0:P]).then_inc(z_taken, 1)
                def half_gate(j):
                    a, _ = unit(f"a{j}")
                    act.activation(th[:, j, :], a[:, :], ACT.Tanh, scale=0.5).then_inc(th_ready, 1)

                def high(e, a, b, unit_name):
                    act.wait_ge(released[g.bank(unit_name)], g.uses_before(unit_name) + 1)
                    act.copy(hidh[e][:, a:b, :], hid[e][:, a:b, :]).then_inc(hid_high[e], 1)

                act.wait_ge(qk_ready, g.count(1, 1))
                act.copy(Q[0:2 * C, :], qk_bank[0:2 * C, :])
                act.copy(Q[2 * C:3 * C, :], qk_bank[0:C, :]).then_inc(qk_high, 1)
                half_gate(0)
                act.copy(K[0:2 * C, :], qk_bank[2 * C:4 * C, :]).then_inc(qk_high, 1)
                for j in range(4):
                    c, free = unit(f"c{j}")
                    act.activation(hid[3][:, j, :], c[:, :], ACT.Gelu, bias=vec(f"ml_b1{j}")).then_inc(free, 1)
                    if first and j == 1:
                        for n in range(FIRST_SPLITS, len(WEIGHT_SPLITS)):
                            high_weights(n)
                act.wait_ge(c_turned, g.count(1, 1))
                act.activation(h2[:, :], TR[:, :], ACT.Identity, bias=vec("n1b"), scale=vec("n1g")) \
                    .then_inc(h2_ready, 1)
                act.wait_ge(h2_ready, g.count(1, 1))
                act.copy(h2h[:, :], h2[:, :]).then_inc(h2_high, 1)
                half_gate(1)
                high(3, 0, 2, "c1")
                high(3, 2, 4, "c3")
                for j in range(2):
                    f, free = unit(f"f1_{j}")
                    act.activation(hid[2][:, j, :], f[:, :], ACT.Relu, bias=vec(f"f1b{j}")).then_inc(free, 1)
                high(2, 0, 2, "f1_1")
                high(0, 0, 2, "b1")
                act.wait_ge(lean_ready, g.count(1, 1))
                act.activation(tlean[:, :, :], lean[:, :, :], ACT.Tanh).then_inc(tlean_ready, 1)
                half_gate(2)
                half_gate(3)
                high(0, 2, 3, "b2")
                expert_copy(g, 1, 3, "ml_b2")
                high(0, 3, 4, "b3")
                if not last:
                    take_x(g.next())
                expert_copy(g, 2, 0, None)
                for j in range(2):
                    m, free = unit(f"m{j}")
                    act.activation(hid[1][:, j, :], m[:, :], ACT.Gelu, bias=me_b[:, j:j + 1]).then_inc(free, 1)

            turns(act, turn, lambda g: None)

        @block.vector
        def _(dve):
            chain = [0]

            def link(ins):
                chain[0] += 1
                ins.then_inc(setup_dve, 1)
                dve.wait_ge(setup_dve, chain[0])

            def x_moments(g):
                dve.wait_ge(x_loaded[g.par], g.half(DMA_INC, DMA_INC))
                for t in range(NT):
                    dve.bn_stats(stats["x"][:, t, :], X[g.par][:, t, :])
                dve.drain()
                for t in range(NT):
                    ins = dve.bn_aggr(mv["x"][:, t, :], stats["x"][:, t, :])
                ins.then_inc(x_stats, 1)

            dve.wait_ge(expo_ready, 3)
            dve.memset(pacc[:, :], 1.0)
            for n in range(7):
                dve.tensor_scalar(bit[:, n, :], expo[:, :], n, 1, ALU.logical_shift_right, ALU.bitwise_and)
            dve.wait_ge(decay_tanh, 1)
            decay_at = [0]

            def decay_steps(count):
                for _ in range(count):
                    kind, n = DECAY_STEPS[decay_at[0]]
                    if decay_at[0] > 0:
                        dve.wait_ge(decay_step, decay_at[0])
                    if kind == "power" and n == 0:
                        ins = dve.tensor_scalar(power[:, 0:1], power[:, 8:9], 0.5, 0.5, ALU.mult, ALU.add)
                    elif kind == "power":
                        ins = dve.tensor_tensor(power[:, n:n + 1], power[:, n - 1:n], power[:, n - 1:n], ALU.mult)
                    elif kind == "times":
                        ins = dve.tensor_scalar(ptry[:, :], pacc[:, :], power[:, n:n + 1], None, ALU.mult)
                    else:
                        ins = dve.copy_predicated(pacc[:, :], bit[:, n, :], ptry[:, :])
                    ins.then_inc(decay_step, 1)
                    decay_at[0] += 1

            decay_steps(2)
            x_moments(Group(0, 0))
            decay_steps(1)
            taken = [0]

            def product(name):
                assert TAKEN[taken[0]] == name
                dve.wait_ge(setup_mm, MM.index(name) + 1)
                taken[0] += 1

            def took(ins):
                ins.then_inc(setup_took, 1)
                dve.wait_ge(setup_took, taken[0])

            dve.wait_ge(vec_loaded, DMA_INC)
            dve.wait_ge(w_loaded[0], DMA_INC)
            link(dve.tensor_tensor(tokb[:, P:P + E], row("router_b"), row("balancer"), ALU.add))
            decay_steps(1)
            product("ce1")
            dve.tensor_scalar(ce_x1[:, P:P + 1], prod("ce1", cols=P + 1)[:, P:P + 1], vec("ce_bv"), None, ALU.add)
            took(dve.tensor_copy(ce_x1[:, 0:P], prod("ce1")))
            decay_steps(2)
            product("qk")
            qk = slice(SPLIT["qk"], SPLIT["qk"] + 4 * C)
            link(dve.tensor_copy(WH[:, qk], prod("qk", cols=4 * C)))
            took(dve.tensor_tensor(WL[:, qk], prod("qk", cols=4 * C), WH[:, qk], ALU.subtract))
            product("ce2")
            link(dve.tensor_tensor(ce_x2[:, :], prod("ce2", cols=P + 1), w("ce_x0"), ALU.add))
            took(dve.tensor_scalar(ce_x2[:, P:P + 1], ce_x2[:, P:P + 1], vec("ce_bo"), None, ALU.add))
            link(dve.tensor_copy(bcast[:, 0, :], ce_x2[:, P:P + 1].broadcast_to([P, P])))
            assert chain[0] == CE_BIAS_LINK
            product("vo")
            took(dve.tensor_copy(tokw[:, 0:P], prod("vo")))
            decay_steps(2)
            product("ce")
            took(dve.tensor_copy(tokw[:, P:2 * P], prod("ce")))
            decay_steps(1)
            product("ce_b")
            took(dve.tensor_copy(tokb[:, 0:P], prod("ce_b")))
            decay_steps(1)

            def x_low(g):
                dve.wait_ge(x_high, g.count(1, 1))
                dve.tensor_tensor(xl[g.par][:, :], TR[:, :], xh[g.par][:, :], ALU.subtract).then_inc(x_split, 1)

            x_low(Group(0, 0))
            decay_steps(4)

            def fold_first():
                dve.wait_ge(w_loaded[LOAD_OF["me_x0"]], DMA_INC)
                product("me1")
                dve.tensor_scalar(me_x1[:, P:P + 1], prod("me1", cols=P + 1)[:, P:P + 1], vec("me_bv"), None, ALU.add)
                took(dve.tensor_copy(me_x1[:, 0:P], prod("me1")))
                product("gen")
                took(dve.tensor_copy(gen_c[:, :], prod("gen")))

            def fold_second():
                product("me2")
                dve.tensor_scalar(me_x2[:, P:P + 1], prod("me2", cols=P + 1)[:, P:P + 1], vec("me_bo"), None, ALU.add)
                took(dve.tensor_copy(me_x2[:, 0:P], prod("me2")))
                product("gen_b")
                took(dve.tensor_tensor(gen_bias[:, :], prod("gen_b"), row("gen_b"), ALU.add))

            def fold_last():
                me = slice(SPLIT["me"], SPLIT["me"] + 2 * P)
                product("me")
                link(dve.tensor_copy(WH[:, me], prod("me", cols=2 * P)))
                took(dve.tensor_tensor(WL[:, me], prod("me", cols=2 * P), WH[:, me], ALU.subtract))
                product("me_b")
                took(dve.tensor_tensor(me_b[:, :], prod("me_b", cols=2),
                                       VEC[:, VECS.index("me_c1b0"):VECS.index("me_c1b0") + 2], ALU.add))

            def finish_mask():
                decay_steps(len(DECAY_STEPS) - decay_at[0])
                dve.wait_ge(decay_step, len(DECAY_STEPS))
                dve.tensor_scalar(mask[:, 0:P], pacc[:, P + 1:PW], pacc[:, P:P + 1], power[:, 8:9],
                                  ALU.mult, ALU.mult)
                dve.tensor_scalar(mask[:, P:2 * P], pacc[:, P + 1:PW], pacc[:, P:P + 1], power[:, 7:8],
                                  ALU.mult, ALU.mult)
                dve.tensor_scalar(mask[:, 2 * P:3 * P], pacc[:, P + 1:PW], pacc[:, P:P + 1], None, ALU.mult)
                link(dve.tensor_scalar(ptry[:, 0:P], expo[:, 0:P], 0.0, None, ALU.is_ge))
                link(dve.tensor_tensor(mask[:, 3 * P:T], pacc[:, 0:P], ptry[:, 0:P], ALU.mult))

            def mix(g, n, e):
                dve.wait_ge(ex_ready, g.count(E, n))
                for t in range(NT):
                    ins = dve.scalar_tensor_tensor(out=OUT[g.par][:, t, :], in0=EX[EX_BANK[e]][:, t, :],
                                                   scalar=coef[g.par][:, t, e:e + 1], in1=OUT[g.par][:, t, :],
                                                   op0=ALU.mult, op1=ALU.add)
                ins.then_inc(ex_taken, 1)

            def expert2_scale(g):
                dve.wait_ge(u_rstd, g.count(1, 1))
                dve.wait_ge(ex_ready, g.count(E, 4))
                for t in range(NT):
                    ins = dve.scalar_tensor_tensor(out=e2[:, t, :], in0=EX[EX_BANK[2]][:, t, :],
                                                   scalar=rstd["u"][:, t:t + 1], in1=gen_bias[:, :],
                                                   op0=ALU.mult, op1=ALU.add)
                ins.then_inc(ex_taken, 1)

            def expert1(g):
                dve.wait_ge(ex_taken, g.count(E, 2))
                mix(g, 3, 1)

            def expert2_add(g):
                dve.wait_ge(ex_taken, g.count(E, 4))
                for t in range(NT):
                    ins = dve.scalar_tensor_tensor(out=OUT[g.par][:, t, :], in0=e2[:, t, :],
                                                   scalar=coef[g.par][:, t, 2:3], in1=OUT[g.par][:, t, :],
                                                   op0=ALU.mult, op1=ALU.add)
                ins.then_inc(out_ready, 1)

            def u_moments(g):
                dve.wait_ge(unit_ready, g.count(NU, NU))
                for t in range(NT):
                    ins = dve.bn_stats(stats["u"][:, t, :], S[g.bank("ut")][:, t * P:(t + 1) * P])
                ins.then_inc(released[g.bank("ut")], 1)

            def u_combine(g):
                dve.drain()
                for t in range(NT):
                    ins = dve.bn_aggr(mv["u"][:, t, :], stats["u"][:, t, :])
                ins.then_inc(u_stats, 1)

            def expert0(g):
                dve.wait_ge(ex_taken, g.count(E, 1))
                mix(g, 2, 0)

            def turn(g, first, last):
                def unit(name):
                    dve.wait_ge(unit_ready, g.count(NU, UNITS.index(name) + 1))
                    return S[g.bank(name)], released[g.bank(name)]

                if not first:
                    u_moments(g.prev())
                for t in range(NT):
                    dve.wait_ge(z_taken, g.count(NT, t + 1))
                    dve.tensor_tensor(pl[:, t, :], S[g.bank(f"tok{t}")][:, P:TOKW], tokb[:, :], ALU.add) \
                        .then_inc(released[g.bank(f"tok{t}")], 1)
                    if first:
                        decay_steps(2)
                for t in range(NT):
                    b = g.bank(f"tok{t}")
                    dve.wait_ge(released[b], g.uses_before(f"tok{t}") + 1)
                    dve.bn_stats(stats["c"][:, t, :], pl[:, t, 0:P])
                dve.drain()
                for t in range(NT):
                    ins = dve.bn_aggr(mv["c"][:, t, :], stats["c"][:, t, :])
                ins.then_inc(c_stats, 1)
                def masked_scores():
                    for s in range(NT):
                        n = (s + 1) * P
                        sc, free = unit(f"sc{s}")
                        dve.tensor_tensor(pr[:, s, 0:n], sc[:, 0:n], mask[:, T - n:T], ALU.mult).then_inc(free, 1)

                def silu(j):
                    dve.wait_ge(th_ready, g.count(4, j + 1))
                    a, a_free = S[g.bank(f"a{j}")], released[g.bank(f"a{j}")]
                    dve.scalar_tensor_tensor(out=gate[:, j, :], in0=th[:, j, :], scalar=1.0, in1=a[:, :],
                                             op0=ALU.add, op1=ALU.mult).then_inc(a_free, 1)
                    b, b_free = unit(f"b{j}")
                    dve.wait_ge(a_free, g.uses_before(f"a{j}") + 1)
                    dve.tensor_tensor(hid[0][:, j, :], gate[:, j, :], b[:, :], ALU.mult).then_inc(b_free, 1)

                dve.wait_ge(qk_high, g.count(2, 1))
                dve.tensor_tensor(Q[C:2 * C, :], qk_bank[C:2 * C, :], Q[C:2 * C, :], ALU.subtract)
                silu(0)
                dve.wait_ge(qk_high, g.count(2, 2))
                dve.tensor_tensor(K[2 * C:3 * C, :], qk_bank[3 * C:4 * C, :], K[C:2 * C, :], ALU.subtract) \
                    .then_inc(qk_split, 1)
                if first:
                    x_moments(g.next())
                    finish_mask()
                masked_scores()
                if first:
                    fold_first()
                if not first:
                    expert0(g.prev())
                    u_combine(g.prev())
                dve.wait_ge(h2_high, g.count(1, 1))
                dve.tensor_tensor(h2l[:, :], h2[:, :], h2h[:, :], ALU.subtract).then_inc(h2_low, 1)
                silu(1)
                if first:
                    fold_second()

                rs = [0]

                def route(ins):
                    rs[0] += 1
                    ins.then_inc(route_step, 1)
                    dve.wait_ge(route_step, g.count(ROUTE_STEPS, rs[0]))

                logit = pl[:, :, P:P + E]
                mine = logit.unsqueeze(3).broadcast_to([P, NT, E, E])
                other = logit.unsqueeze(2).broadcast_to([P, NT, E, E])
                route(dve.tensor_tensor(same[:, :, :, :], other, mine, ALU.is_equal))
                route(dve.tensor_tensor(same[:, :, :, :], same[:, :, :, :],
                                        earlier[:, :, :].unsqueeze(1).broadcast_to([P, NT, E, E]), ALU.mult))
                route(dve.tensor_tensor(more[:, :, :, :], other, mine, ALU.is_gt))
                route(dve.tensor_tensor(more[:, :, :, :], more[:, :, :, :], same[:, :, :, :], ALU.add))
                route(dve.tensor_reduce(rank[:, :, :], more[:, :, :, :], AX.X, ALU.add))
                route(dve.scalar_tensor_tensor(out=top[:, :, :], in0=rank[:, :, :], scalar=1.5, in1=logit,
                                               op0=ALU.is_lt, op1=ALU.mult))
                route(dve.tensor_reduce(topsum[:, :], top[:, :, :], AX.X, ALU.add))
                dve.scalar_tensor_tensor(out=lean[:, :, :], in0=topsum[:, :].unsqueeze(2).broadcast_to([P, NT, E]),
                                         scalar=-0.5, in1=logit, op0=ALU.mult, op1=ALU.add).then_inc(lean_ready, 1)
                route(dve.tensor_scalar(half[:, :, :], rank[:, :, :], 1.5, 0.5, ALU.is_lt, ALU.mult))

                if not first:
                    expert1(g.prev())
                    expert2_scale(g.prev())
                wait(dve, out_stored[g.par], g.half(DMA_INC, 0))
                dve.wait_ge(att_ready, g.count(1, 1))
                dve.tensor_tensor(OUT[g.par][:, :, :], ATT[:, :, :], X[g.par][:, :, :], ALU.add) \
                    .then_inc(att_added, 1)
                if first:
                    fold_last()
                silu(2)
                dve.wait_ge(tlean_ready, g.count(1, 1))
                route(dve.scalar_tensor_tensor(out=coef[g.par][:, :, :], in0=tlean[:, :, :], scalar=1.0,
                                               in1=half[:, :, :], op0=ALU.add, op1=ALU.mult))
                assert rs[0] == ROUTE_STEPS
                silu(3)
                if not first:
                    expert2_add(g.prev())
                f2, free = unit("f2")
                dve.scalar_tensor_tensor(out=u[:, :], in0=f2[:, :], scalar=vec("f2b"), in1=h2[:, :],
                                         op0=ALU.add, op1=ALU.add).then_inc(free, 1)
                dve.wait_ge(att_added, g.count(1, 1))
                for t in range(NT):
                    ins = dve.scalar_tensor_tensor(out=OUT[g.par][:, t, :], in0=row("me_c2b"),
                                                   scalar=coef[g.par][:, t, 1:2], in1=OUT[g.par][:, t, :],
                                                   op0=ALU.mult, op1=ALU.add)
                ins.then_inc(bias1_added, 1)
                if not last:
                    x_low(g.next())
                dve.wait_ge(bias1_added, g.count(1, 1))
                mix(g, 1, 3)
                if two_more(g):
                    x_moments(Group(g.pair, g.off + 2))

            def tail(g):
                u_moments(g)
                u_combine(g)
                expert0(g)
                expert1(g)
                expert2_scale(g)
                expert2_add(g)

            turns(dve, turn, tail)

        @block.tensor
        def _(pe):
            done = [0]

            def setup(name, n_out, lhsT, rhs, rows_=P):
                assert MM[done[0]] == name
                before = [n for n in range(done[0]) if bank_of[n] == bank_of[done[0]]]
                if before:
                    after(MM[before[-1]])
                pe.matmul(prod(name, rows_, n_out), lhsT, rhs, start=True, stop=True).then_inc(setup_mm, 1)
                done[0] += 1

            def after(name):
                pe.wait_ge(setup_took, TAKEN.index(name) + 1)

            pe.wait_ge(w_loaded[0], DMA_INC)
            setup("ce1", P + 1, w("ce_wv"), w("ce_x0"))
            setup("vT", P, w("vcT"), w("basisT"), C)
            setup("oT", P, w("ocT"), w("basisT"), C)
            setup("qk", 4 * C, w("basisT"), w("qkT"))
            after("ce1")
            setup("ce2", P + 1, w("ce_wo"), ce_x1[:, :])
            pe.wait_ge(setup_act, 2)
            setup("vo", P, vT[:, :], oT[:, :])

            def turn_x(g):
                for t in range(NT):
                    pe.wait_ge(x_normed, g.count(NT, t + 1))
                    ins = pe.transpose(TR[:, t * P:(t + 1) * P], xn[:, t, :], ident[:, :])
                ins.then_inc(x_turned, 1)

            pe.wait_ge(pool_const, POOL_CONSTS)
            turn_x(Group(0, 0))
            after("ce2")
            setup("ce", P, ce_x2[:, 0:P], ident[:, :])
            pe.wait_ge(setup_dve, CE_BIAS_LINK)
            setup("ce_b", P, bcast[:, 0, :], ident[:, :])

            def fold_first():
                pe.wait_ge(w_loaded[LOAD_OF["me_x0"]], DMA_INC)
                setup("me1", P + 1, w("me_wv"), w("me_x0"))
                pe.wait_ge(setup_act, ACT_SETUP)
                setup("gen", P, center[:, :], gen_s[:, :])

            def fold_second():
                after("me1")
                setup("me2", P + 1, w("me_wo"), me_x1[:, :])
                setup("gen_b", P, bcast[:, 1, :], w("gen_w"))

            def fold_last():
                after("me2")
                setup("me", 2 * P, me_x2[:, 0:P], w("me_c1w"))
                after("gen_b")
                for j in range(2):
                    ins = pe.matmul(flat[bank_of[MM.index("me_b")]][:, j:j + 1], w("me_c1w", j * P, P),
                                    me_x2[:, P:P + 1], start=True, stop=True)
                ins.then_inc(setup_mm, 1)

            pe.wait_ge(setup_act, 3)
            after("ce_b")

            def expert_sum(g, e, parts, col):
                bank = EX[EX_BANK[e]][:, :, :].rearrange("p t n -> p (t n)")
                for j in range(parts):
                    pe.wait_ge(hid_low[e], g.count(parts, j + 1))
                    wh, wl = WH[:, col + j * P:col + (j + 1) * P], WL[:, col + j * P:col + (j + 1) * P]
                    pe.matmul(bank, wh, hidh[e][:, j, :], start=(j == 0), stop=False)
                    pe.matmul(bank, wh, hidl[e][:, j, :], start=False, stop=False)
                    ins = pe.matmul(bank, wl, hidh[e][:, j, :], start=False, stop=(j == parts - 1))
                ins.then_inc(ex_summed, 1)

            def expert1(g):
                pe.wait_ge(ex_taken, g.count(E, 1))
                b = g.bank("m1")
                pe.wait_ge(released[b], g.uses_before("m1") + 1)
                for t in range(NT):
                    for j in range(2):
                        ins = pe.matmul(EX[EX_BANK[1]][:, t, :], hid[1][:, j, t * P:(t + 1) * P],
                                        w("me_c2w", j * P, P), start=(j == 0), stop=(j == 1))
                ins.then_inc(ex_ready, 1)

            def expert2(g):
                pe.wait_ge(ex_taken, g.count(E, 2))
                for t in range(NT):
                    ins = pe.matmul(EX[EX_BANK[2]][:, t, :], u[:, t * P:(t + 1) * P], gen_c[:, :],
                                    start=True, stop=True)
                ins.then_inc(ex_ready, 1)

            def expert_turn(g, n, e):
                pe.wait_ge(ex_copied, g.count(2, n))
                for t in range(NT):
                    ins = pe.transpose(EX[EX_BANK[e]][:, t, :], exT[:, t * P:(t + 1) * P], ident[:, :])
                ins.then_inc(ex_ready, 1)

            def turn(g, first, last):
                def fill(name):
                    wait(pe, released[g.bank(name)], g.uses_before(name))
                    return S[g.bank(name)]

                def three(name, col, hi, lo):
                    bank = fill(name)
                    wh, wl = WH[:, col:col + P], WL[:, col:col + P]
                    pe.matmul(bank[:, :], wh, hi, start=True, stop=False)
                    pe.matmul(bank[:, :], wh, lo, start=False, stop=False)
                    pe.matmul(bank[:, :], wl, hi, start=False, stop=True).then_inc(unit_ready, 1)

                h, l, full = xh[g.par][:, :], xl[g.par][:, :], xT[g.par]

                pe.wait_ge(x_high, g.count(1, 1))
                for t in range(NT):
                    bank = fill(f"tok{t}")
                    pe.matmul(bank[:, 0:TOKW], full[:, t * P:(t + 1) * P], tokw[:, :], start=True, stop=True) \
                        .then_inc(unit_ready, 1)
                wait(pe, att_added, g.count(1, 0))
                pe.wait_ge(x_split, g.count(1, 1))
                wh, wl = (m[:, SPLIT["qk"]:SPLIT["qk"] + 4 * C] for m in (WH, WL))
                pe.matmul(qk_bank, wh, h, start=True, stop=False)
                pe.matmul(qk_bank, wh, l, start=False, stop=False)
                pe.matmul(qk_bank, wl, h, start=False, stop=True).then_inc(qk_ready, 1)

                def gates(j):
                    three(f"a{j}", SPLIT["w1"] + j * P, h, l)
                    three(f"b{j}", SPLIT["w3"] + j * P, h, l)

                if first:
                    fold_first()
                    pe.wait_ge(split_low, 1)
                gates(0)
                if first:
                    pe.wait_ge(split_low, 2)
                for j in range(4):
                    if j == 2 and not first:
                        expert_turn(g.prev(), 2, 0)
                    three(f"c{j}", SPLIT["ml"] + j * P, h, l)
                pe.wait_ge(qk_split, g.count(1, 1))
                for s in range(NT):
                    if s == NT - 1:
                        for t in range(NT):
                            pe.wait_ge(c_normed, g.count(NT, t + 1))
                            ins = pe.transpose(TR[:, t * P:(t + 1) * P], n1[:, t, :], ident[:, :])
                        ins.then_inc(c_turned, 1)
                    bank = fill(f"sc{s}")
                    pe.matmul(bank[:, 0:(s + 1) * P], K[:, s * P:(s + 1) * P], Q[:, 0:(s + 1) * P],
                              start=True, stop=True).then_inc(unit_ready, 1)
                gates(1)
                if first:
                    fold_second()
                else:
                    expert1(g.prev())
                    expert2(g.prev())
                pe.wait_ge(h2_low, g.count(1, 1))
                three("f1_0", SPLIT["f1"], h2h[:, :], h2l[:, :])
                three("f1_1", SPLIT["f1"] + P, h2h[:, :], h2l[:, :])
                b = g.bank(f"sc{NT - 1}")
                pe.wait_ge(released[b], g.uses_before(f"sc{NT - 1}") + 1)
                for t in range(NT):
                    for s in range(t, NT):
                        ins = pe.matmul(ATT[:, t, :], pr[:, s, t * P:(t + 1) * P], z[:, s, :],
                                        start=(s == t), stop=(s == NT - 1))
                ins.then_inc(att_ready, 1)
                if first:
                    fold_last()
                gates(2)
                gates(3)
                if first:
                    pe.wait_ge(setup_took, len(TAKEN))
                    pe.wait_ge(split_low, len(WEIGHT_SPLITS))
                else:
                    pe.wait_ge(ex_taken, g.prev().count(E, 3))
                expert_sum(g, 3, 4, SPLIT["ml2"])
                bank = fill("f2")
                for j in range(2):
                    pe.wait_ge(hid_low[2], g.count(2, j + 1))
                    wh, wl = (m[:, SPLIT["f2"] + j * P:SPLIT["f2"] + (j + 1) * P] for m in (WH, WL))
                    pe.matmul(bank[:, :], wh, hidh[2][:, j, :], start=(j == 0), stop=False)
                    pe.matmul(bank[:, :], wh, hidl[2][:, j, :], start=False, stop=False)
                    ins = pe.matmul(bank[:, :], wl, hidh[2][:, j, :], start=False, stop=(j == 1))
                ins.then_inc(unit_ready, 1)
                pe.wait_ge(h2_ready, g.count(1, 1))
                if not last:
                    turn_x(g.next())
                expert_turn(g, 1, 3)
                if not first:
                    pe.wait_ge(ex_taken, g.prev().count(E, 4))
                expert_sum(g, 0, 4, SPLIT["sw2"])
                three("m0", SPLIT["me"], h, l)
                three("m1", SPLIT["me"] + P, h, l)
                b = g.bank("f2")
                pe.wait_ge(released[b], g.uses_before("f2") + 1)
                bank = fill("ut")
                for t in range(NT):
                    ins = pe.transpose(bank[:, t * P:(t + 1) * P], u[:, t * P:(t + 1) * P], ident[:, :])
                ins.then_inc(unit_ready, 1)

            def tail(g):
                expert_turn(g, 2, 0)
                expert1(g)
                expert2(g)

            turns(pe, turn, tail)


ROUTE_STEPS = 9
DECAY_STEPS = ([("power", 0), ("power", 1), ("times", 0), ("power", 2), ("take", 0)]
               + [s for n in range(1, 7) for s in (("power", n + 2), ("times", n), ("take", n))])
POOL_CONSTS = 10
CE_BIAS_LINK = 4
ACT_SETUP = 5


def kernel(**inputs):
    import numpy as np
    import concourse.bacc as bacc
    from concourse.bass_utils import run_bass_kernel_spmd

    a = {k[7:] if k.startswith("L0_ffn_") else k: np.asarray(v) for k, v in inputs.items()}

    def chunks(m):
        return np.concatenate([m[j * P:(j + 1) * P] for j in range(m.shape[0] // P)], axis=1)

    basis_t = a["L0_attn_basis"].T
    q, k = a["L0_attn_q_coeffs"].T, a["L0_attn_k_coeffs"].T
    packed = {
        "basisT": basis_t, "qkT": np.concatenate([q, q, k, k], axis=1),
        "vcT": a["L0_attn_v_coeffs"].T, "ocT": a["L0_attn_o_coeffs"].T,
        "ce_x0": np.concatenate([a["ce_syn_w"].T, a["ce_syn_b"][:, None]], axis=1),
        "ce_wv": a["ce_wv"], "ce_wo": a["ce_wo"], "router": a["router_w"], "gen_w": a["ce_gen_w"],
        "sw_w1": a["sw_w1"], "sw_w3": a["sw_w3"],
        "me_x0": np.concatenate([a["me_eq_w"].T, a["me_eq_b"][:, None]], axis=1),
        "me_wv": a["me_wv"], "me_wo": a["me_wo"], "me_c1w": a["me_c1w"],
        "ml_w1": a["ml_w1"], "f1w": a["ce_f1w"],
        "f2w": chunks(a["ce_f2w"]), "sw_w2": chunks(a["sw_w2"]), "me_c2w": chunks(a["me_c2w"]),
        "ml_w2": chunks(a["ml_w2"]),
    }
    weights = np.concatenate([packed[name] for load in LOADS for name, _ in load], axis=1)
    c1b, f1b, mlb = (a[n].reshape(-1, P) for n in ("me_c1b", "ce_f1b", "ml_b1"))
    vecs = {"me_bv": a["me_bv"], "me_bo": a["me_bo"], "me_c1b0": c1b[0], "me_c1b1": c1b[1],
            "ce_bv": a["ce_bv"], "ce_bo": a["ce_bo"], "n1g": a["ce_n1g"], "n1b": a["ce_n1b"],
            "f1b0": f1b[0], "f1b1": f1b[1], "f2b": a["ce_f2b"], "n2g": a["ce_n2g"], "n2b": a["ce_n2b"],
            "ml_b10": mlb[0], "ml_b11": mlb[1], "ml_b12": mlb[2], "ml_b13": mlb[3],
            "ml_b2": a["ml_b2"]}
    row = np.concatenate([a["ce_gen_b"], a["router_b"], a["load_balancer"],
                          a["L0_attn_decay_logit"].reshape(1), a["L0_attn_out_scale"].reshape(1),
                          a["me_c2b"]])
    arrays = {
        "x": np.ascontiguousarray(a["L0_attn_x"]),
        "weights": np.ascontiguousarray(weights),
        "vecs": np.ascontiguousarray(np.stack([vecs[n] for n in VECS], axis=1)),
        "rows": np.ascontiguousarray(row[None, :]),
    }
    nc = bacc.Bacc("TRN2", target_bir_lowering=False, num_devices=1)
    args = [nc.dram_tensor(n, v.shape, mybir.dt.from_np(v.dtype), kind="ExternalInput").ap()
            for n, v in arrays.items()]
    out = nc.dram_tensor("out", (GROUPS, T, P), F32, kind="ExternalOutput").ap()
    build(nc, *args, out)
    r = run_bass_kernel_spmd(nc, [arrays], core_ids=[0])
    return r.results[0]["out"]
```
